# Optimizing a Trainium2 kernel written in Bass

```python
import numpy as np
import jax
import jax.numpy as jnp

def _softmax(x, axis=-1):
    return jax.nn.softmax(x, axis=axis)

def _gelu(x):
    return jax.nn.gelu(x, approximate=True)

def _silu(x):
    return jax.nn.silu(x)

def _sigmoid(x):
    return jax.nn.sigmoid(x)

def _layernorm(x, axis=-1, eps=1e-05):
    m = jnp.mean(x, axis=axis, keepdims=True)
    v = jnp.var(x, axis=axis, keepdims=True)
    return (x - m) / jnp.sqrt(v + eps)

def _scatter_add(tgt, idx, src, axis=0):
    return tgt.at[idx].add(src)

def _segment_sum(src, seg, n):
    return jax.ops.segment_sum(src, seg, n)
kernel_name = 'mk_perceiver_d1_seqx_r2_7561ce'

def setup_inputs(seed: int=0):
    np.random.seed(seed)
    _w = jnp.asarray

    def _rec_inputs():
        import jax
        import jax.numpy as jnp
        _rk = jax.random.key(seed)
        x = -0.0002928 + 1 * jax.random.normal(jax.random.fold_in(_rk, 1), (2, 128, 512), jnp.float32)
        _lenS = 128 - jax.random.randint(jax.random.fold_in(_rk, 7), (2,), 0, max(1, 128 // 4) + 1, jnp.int32)
        _lenS2 = 2048 - jax.random.randint(jax.random.fold_in(_rk, 8), (2,), 0, max(1, 2048 // 4) + 1, jnp.int32)
        _ctx_1024P = jax.random.normal(jax.random.fold_in(_rk, 11), (2, 16, 512), jnp.float32)
        _ctx_1024c = jax.random.dirichlet(jax.random.fold_in(_rk, 511), 0.3 * jnp.ones((16,), jnp.float32), (2, 2048))
        _ctx_1024t = jnp.einsum('bsk,bkd->bsd', _ctx_1024c, _ctx_1024P)
        _ctx_1024t = _ctx_1024t * jax.lax.rsqrt(jnp.mean(jnp.square(_ctx_1024t)) + 1e-12) * 0.953939
        ctx_1024 = -1.39393e-06 + 0.999914 * (_ctx_1024t + 0.3 * jax.random.normal(jax.random.fold_in(_rk, 611), (2, 2048, 512), jnp.float32))
        return (x, ctx_1024)
    x, ctx_1024 = _rec_inputs()

    def _L0_xattn_setup():
        import jax, jax.numpy as jnp
        import numpy as np
        D_MODEL = 512
        N_HEAD = 16
        D_HEAD = D_MODEL // N_HEAD
        B, Q, K = (2, 1024, 1024)
        key = jax.random.key(seed)
        ks = jax.random.split(key, 11)
        s = 1.0 / np.sqrt(D_MODEL)
        return {'q': jax.random.normal(ks[0], (B, Q, D_MODEL), jnp.float32), 'k': jax.random.normal(ks[1], (B, K, D_MODEL), jnp.float32), 'v': jax.random.normal(ks[2], (B, K, D_MODEL), jnp.float32), 'Wq': jax.random.normal(ks[3], (D_MODEL, D_MODEL), jnp.float32) * s, 'bq': jnp.zeros((D_MODEL,), jnp.float32), 'Wk': jax.random.normal(ks[4], (D_MODEL, D_MODEL), jnp.float32) * s, 'bk': jnp.zeros((D_MODEL,), jnp.float32), 'Wv': jax.random.normal(ks[5], (D_MODEL, D_MODEL), jnp.float32) * s, 'bv': jnp.zeros((D_MODEL,), jnp.float32), 'Wo': jax.random.normal(ks[6], (D_MODEL, D_MODEL), jnp.float32) * s, 'bo': jnp.zeros((D_MODEL,), jnp.float32)}
    _L0_xattn_all = _L0_xattn_setup()
    _L0_xattn_in = {k: v for k, v in _L0_xattn_all.items() if k in ('Wq', 'bq', 'Wk', 'bk', 'Wv', 'bv', 'Wo', 'bo')}
    del _L0_xattn_all

    def _L0_attn_setup():
        import jax, jax.numpy as jnp
        import numpy as np
        DIMS = 512
        HEADS = 16
        HEAD_DIM = DIMS // HEADS
        key = jax.random.key(seed)
        k_x, k_q, k_k, k_v = jax.random.split(key, 4)
        scale = 1.0 / np.sqrt(DIMS)
        return {'input_seq_embs': jax.random.normal(k_x, (4, 2048, DIMS), dtype=jnp.float32), 'W_Q': jax.random.normal(k_q, (DIMS, DIMS), dtype=jnp.float32) * scale, 'W_K': jax.random.normal(k_k, (DIMS, DIMS), dtype=jnp.float32) * scale, 'W_V': jax.random.normal(k_v, (DIMS, DIMS), dtype=jnp.float32) * scale}
    _L0_attn_all = _L0_attn_setup()
    _L0_attn_in = {k: v for k, v in _L0_attn_all.items() if k in ('W_Q', 'W_K', 'W_V')}
    del _L0_attn_all

    def _L0_ffn_setup():
        import jax, jax.numpy as jnp
        import numpy as np
        DIM = 512

        def _reference_tuple_inner(x, W_r, W_k, W_v, mu_r, mu_k):
            B, T, C = x.shape
            x_prev = jnp.concatenate([jnp.zeros((B, 1, C), x.dtype), x[:, :-1, :]], axis=1)
            xr = mu_r * x + (1.0 - mu_r) * x_prev
            xk = mu_k * x + (1.0 - mu_k) * x_prev
            r = jax.nn.sigmoid(jnp.einsum('btc,dc->btd', xr, W_r))
            k = jnp.einsum('btc,dc->btd', xk, W_k)
            k_act = jnp.square(jax.nn.relu(k))
            out = r * jnp.einsum('btc,dc->btd', k_act, W_v)
            new_state = x[:, -1, :]
            return (out, new_state)
        key = jax.random.key(seed)
        ks = jax.random.split(key, 6)
        B, T, C = (8, 1024, DIM)
        x = jax.random.normal(ks[0], (B, T, C), dtype=jnp.float32)
        s = 1.0 / np.sqrt(C)
        W_r = jax.random.uniform(ks[1], (C, C), jnp.float32, -s, s)
        W_k = jax.random.uniform(ks[2], (C, C), jnp.float32, -s, s)
        W_v = jax.random.uniform(ks[3], (C, C), jnp.float32, -s, s)
        mu_r = jax.random.uniform(ks[4], (C,), jnp.float32)
        mu_k = jax.random.uniform(ks[5], (C,), jnp.float32)
        return {'x': x, 'W_r': W_r, 'W_k': W_k, 'W_v': W_v, 'mu_r': mu_r, 'mu_k': mu_k}
    _L0_ffn_all = _L0_ffn_setup()
    _L0_ffn_in = {k: v for k, v in _L0_ffn_all.items() if k in ('W_r', 'W_k', 'W_v', 'mu_r', 'mu_k')}
    del _L0_ffn_all
    return {'x': x, 'ctx_1024': ctx_1024, 'L0_xattn_Wq': _L0_xattn_in['Wq'], 'L0_xattn_bq': _L0_xattn_in['bq'], 'L0_xattn_Wk': _L0_xattn_in['Wk'], 'L0_xattn_bk': _L0_xattn_in['bk'], 'L0_xattn_Wv': _L0_xattn_in['Wv'], 'L0_xattn_bv': _L0_xattn_in['bv'], 'L0_xattn_Wo': _L0_xattn_in['Wo'], 'L0_xattn_bo': _L0_xattn_in['bo'], 'L0_attn_W_Q': _L0_attn_in['W_Q'], 'L0_attn_W_K': _L0_attn_in['W_K'], 'L0_attn_W_V': _L0_attn_in['W_V'], 'L0_ffn_W_r': _L0_ffn_in['W_r'], 'L0_ffn_W_k': _L0_ffn_in['W_k'], 'L0_ffn_W_v': _L0_ffn_in['W_v'], 'L0_ffn_mu_r': _L0_ffn_in['mu_r'], 'L0_ffn_mu_k': _L0_ffn_in['mu_k']}

def reference(x, ctx_1024, L0_xattn_Wq, L0_xattn_bq, L0_xattn_Wk, L0_xattn_bk, L0_xattn_Wv, L0_xattn_bv, L0_xattn_Wo, L0_xattn_bo, L0_attn_W_Q, L0_attn_W_K, L0_attn_W_V, L0_ffn_W_r, L0_ffn_W_k, L0_ffn_W_v, L0_ffn_mu_r, L0_ffn_mu_k):
    import jax
    import jax.numpy as jnp

    def _L0_xattn_ref(q, k, v, Wq, bq, Wk, bk, Wv, bv, Wo, bo):
        import jax, jax.numpy as jnp
        import numpy as np
        D_MODEL = 512
        N_HEAD = 16
        D_HEAD = D_MODEL // N_HEAD
        B, Q, K = (2, 1024, 1024)
        Bq, Qlen, D = q.shape
        Klen = k.shape[1]
        qh = (q @ Wq + bq).reshape(Bq, Qlen, N_HEAD, D_HEAD).transpose(0, 2, 1, 3)
        kh = (k @ Wk + bk).reshape(Bq, Klen, N_HEAD, D_HEAD).transpose(0, 2, 1, 3)
        vh = (v @ Wv + bv).reshape(Bq, Klen, N_HEAD, D_HEAD).transpose(0, 2, 1, 3)
        logits = jnp.einsum('bhqd,bhkd->bhqk', qh, kh) / np.sqrt(D_HEAD).astype(np.float32)
        attn = jax.nn.softmax(logits, axis=-1)
        out = jnp.einsum('bhqk,bhkd->bhqd', attn, vh)
        out = out.transpose(0, 2, 1, 3).reshape(Bq, Qlen, D)
        return out @ Wo + bo

    def _L0_attn_ref(input_seq_embs, W_Q, W_K, W_V):
        import jax, jax.numpy as jnp
        import numpy as np
        DIMS = 512
        HEADS = 16
        HEAD_DIM = DIMS // HEADS
        B, L, d = input_seq_embs.shape
        H, hd = (HEADS, HEAD_DIM)
        Q = (input_seq_embs @ W_Q.T).reshape(B, L, H, hd)
        K = (input_seq_embs @ W_K.T).reshape(B, L, H, hd)
        V = (input_seq_embs @ W_V.T).reshape(B, L, H, hd)
        sK = jax.nn.softmax(jnp.swapaxes(K, -1, -2), axis=-1)
        tran_V = jnp.einsum('bldh,blhe->blde', sK, V)
        out = jnp.einsum('blhd,blde->blhe', jax.nn.softmax(Q, axis=-1), tran_V)
        return out.reshape(B, L, d)

    def _L0_ffn_ref(x, W_r, W_k, W_v, mu_r, mu_k):
        import jax, jax.numpy as jnp
        import numpy as np
        DIM = 512

        def _reference_tuple_inner(x, W_r, W_k, W_v, mu_r, mu_k):
            B, T, C = x.shape
            x_prev = jnp.concatenate([jnp.zeros((B, 1, C), x.dtype), x[:, :-1, :]], axis=1)
            xr = mu_r * x + (1.0 - mu_r) * x_prev
            xk = mu_k * x + (1.0 - mu_k) * x_prev
            r = jax.nn.sigmoid(jnp.einsum('btc,dc->btd', xr, W_r))
            k = jnp.einsum('btc,dc->btd', xk, W_k)
            k_act = jnp.square(jax.nn.relu(k))
            out = r * jnp.einsum('btc,dc->btd', k_act, W_v)
            new_state = x[:, -1, :]
            return (out, new_state)
        return _reference_tuple_inner(x, W_r, W_k, W_v, mu_r, mu_k)[0]
    x = x + _L0_xattn_ref(_layernorm(x, axis=-1), ctx_1024, ctx_1024, L0_xattn_Wq, L0_xattn_bq, L0_xattn_Wk, L0_xattn_bk, L0_xattn_Wv, L0_xattn_bv, L0_xattn_Wo, L0_xattn_bo)
    x = x + _L0_attn_ref(_layernorm(x, axis=-1), L0_attn_W_Q, L0_attn_W_K, L0_attn_W_V)
    x = x + _L0_ffn_ref(_layernorm(x, axis=-1), L0_ffn_W_r, L0_ffn_W_k, L0_ffn_W_v, L0_ffn_mu_r, L0_ffn_mu_k)
    return x

_drawn_inputs = setup_inputs


def setup_inputs(seed=0):
    import zlib

    import numpy as np

    out = dict(_drawn_inputs(seed))
    spreads = {'L0_xattn_bq': (0.0, 0.403),
     'L0_xattn_bk': (0.0, 0.8),
     'L0_xattn_bv': (0.0, 0.1),
     'L0_xattn_bo': (0.0, 0.1)}
    factors = {'L0_ffn_W_r': 3.149, 'L0_ffn_mu_r': 7.721}
    for name, (base, spread) in spreads.items():
        noise = np.random.default_rng([zlib.crc32(name.encode()), seed]).standard_normal(out[name].shape)
        drawn = base * np.exp(spread * noise) if base else spread * noise
        out[name] = jnp.asarray(drawn.astype(out[name].dtype))
    for name, factor in factors.items():
        out[name] = (out[name] * factor).astype(out[name].dtype)
    return out
```

```python
from contextlib import ExitStack

import concourse.bass as bass
from concourse import mybir

F32 = mybir.dt.float32
F32R = mybir.dt.float32r
BF16 = mybir.dt.bfloat16
F16 = mybir.dt.float16
ALU = mybir.AluOpType
ACT = mybir.ActivationFunctionType
AX_X = mybir.AxisListType.X

P = 128
B = 2
LQ = 128
D = 512
KT = D // P
LK = 2048
H = 16
HD = D // H
MT = D // P
HPT = P // HD
CH = 512
NCH = LK // CH
TT = CH // P
NKT = LK // P
UNITS = TT + MT
VC = 3 * HD + 1
SR = 3 * HD
SM = SR + 2
HALF = NKT // 2
FH = HALF * LQ
TG = P // H
NG = LQ // TG
EPS = 1e-5
SCALE = 1.0 / HD ** 0.5
LIFT = 14 * 0.6931471805599453 / SCALE


def perceiver(nc, x, ctx_t, wq, wk, wv, wo, w_q, w_k, w_v, f_r, f_k, f_v, cols, rows, ident, mask, out):
    v_dram = nc.dram_tensor("v_rows", [B, LQ, D], F32, kind="Internal").ap()
    o_dram = nc.dram_tensor("mixed_rows", [B, LQ, D], F32, kind="Internal").ap()

    with ExitStack() as ctx:
        def sem(name):
            return ctx.enter_context(nc.semaphore(name))

        base = (nc.sbuf_base + 31) // 32 * 32
        at = [base]

        def place(name, shape, dt, size=None):
            n = 1
            for s in shape[1:]:
                n *= s
            n *= 2 if dt in (BF16, F16) else 4
            t = nc.alloc_sbuf_tensor_at(name, shape, dt, offset=at[0])
            at[0] += (n + 31) // 32 * 32
            return t

        k_hi = place("k_hi", [P, MT, LK], F32R)
        k_lo = place("k_lo", [P, MT, LK], F32R)
        v_at = at[0]
        v_parts = place("v_parts", [P, NKT, H, VC], BF16)
        w_at = at[0]
        wk_hi = place("wk_hi", [P, KT, D], F32R)
        wk_lo = place("wk_lo", [P, KT, D], F32R)
        wv_hi = place("wv_hi", [P, KT, D], F32R)
        wv_lo = place("wv_lo", [P, KT, D], F32R)
        both_at = at[0]
        c_hi = place("c_hi", [P, 2, KT, CH], F32R)
        c_lo = place("c_lo", [P, 2, KT, CH], F32R)
        c_raw = place("c_raw", [P, KT, CH], F32)
        q_hi = place("q_hi", [P, D], F32R)
        q_lo = place("q_lo", [P, D], F32R)
        both_end = at[0]
        at[0] = both_at
        k_stack = place("k_stack", [P, 3, LK], F32R)
        p_full = place("p_full", [P, 2, FH], F32)
        p_hi = place("p_hi", [P, 3, FH], F16)
        p_lo = place("p_lo", [P, 3, FH], F16)
        assert at[0] <= both_end
        at[0] = both_end
        q_stack = place("q_stack", [P, H, LQ], F32R)
        qa = place("qa", [P, B, D], F32)
        r1 = place("r1", [P, 2, D], F32)
        id32 = place("id32", [P, P], F32)
        id_r = place("id_r", [P, P], F32R)
        m_cols = place("m_cols", [P, 2, P], F32R)
        colt = place("colt", [P, 4, KT], F32)
        om = place("om", [P, 2, KT], F32)
        stat = place("stat", [P, 2, 6], F32)
        mv = place("mv", [P, 2, 2], F32)
        std = place("std", [P, 2], F32)
        rstd = place("rstd", [P, 2], F32)
        eps = place("eps", [P, 1], F32)
        pm = place("pm", [P, 4], F32)
        m_q = place("m_q", [P, 1], F32)
        rec = place("rec", [P, 4], F32)
        assert at[0] <= nc.sbuf_top, (at[0], nc.sbuf_top)

        at[0] = v_at
        w_raw = place("w_raw", [P, 2, KT, D], F32)
        wq_sb = place("wq_sb", [P, KT, D], F32)
        x_in = place("x_in", [P, B, D], F32)
        xn0 = place("xn0", [P, B, D], F32)
        xn0_t = place("xn0_t", [P, KT, B, LQ], F32)
        assert at[0] <= w_at
        at[0] = base
        names = ["wo_sb", "w_q_sb", "w_k_sb", "w_v_sb", "f_k_sb", "f_r_sb", "f_v_sb"]
        wo_sb, w_q_sb, w_k_sb, w_v_sb, f_k_sb, f_r_sb, f_v_sb = [place(n, [P, KT, D], F32) for n in names]
        assert at[0] <= v_at
        at[0] = w_at
        x_res = place("x_res", [P, B, D], F32)
        bias_rows = place("bias_rows", [P, 2, D], F32)
        maskt = place("maskt", [P, 4, P], F32)
        xo = place("xo", [P, B, D], F32)
        a_t = place("a_t", [P, B, D], F32)
        x1 = place("x1", [P, B, D], F32)
        xn1 = place("xn1", [P, B, D], F32)
        xn1_t = place("xn1_t", [P, B, KT, LQ], F32)
        assert at[0] <= both_at
        vs = place("vs", [P, B, NG, HD], F32)
        og = place("og", [P, B, NG, HD], F32)
        o2 = place("o2", [P, B, D], F32)
        x2 = place("x2", [P, B, D], F32)
        xn2 = place("xn2", [P, B, D], F32)
        xp_t = place("xp_t", [P, KT, B, LQ + 1], F32)
        prev = place("prev", [P, 2, KT, B, LQ], F32)
        assert at[0] <= both_end
        at[0] = v_at
        g_m = place("g_m", [P, B, NG, P], F32)
        q_t = place("q_t", [HD, B, LQ, H], F32)
        k_t = place("k_t", [HD, B, LQ, H], F32)
        assert at[0] <= w_at
        at[0] = v_at
        xr = place("xr", [P, KT, B, LQ], F32)
        xk = place("xk", [P, KT, B, LQ], F32)
        relu = place("relu", [P, MT, B, LQ], F32)
        ka = place("ka", [P, MT, B, LQ], F32)
        assert at[0] <= v_at + 16384
        at[0] = both_end
        gate = place("gate", [P, B, D], F32)
        fin = place("fin", [P, B, D], F32)
        at[0] = base + 7 * 8192
        a_tt = place("a_tt", [P, B, KT, LQ], F32)
        v_sb = place("v_sb", [P, B, D], F32)
        assert at[0] <= v_at
        at[0] = both_end + 8192
        sq = place("sq", [P, B, D], F32)
        sk = place("sk", [P, B, D], F32)
        at[0] = both_end + 8192 + 8192 + 512
        mx = place("mx", [P, B, 48], F32)
        sm = place("sm", [P, B, 48], F32)
        rs = place("rs", [P, B, 48], F32)

        ps = ctx.enter_context(nc.psum_tensor("ps", [P, 8, 512], F32))

        in_x, in_wq, in_wk, in_wv = sem("in_x"), sem("in_wq"), sem("in_wk"), sem("in_wv")
        in_small = sem("in_small")
        in_chunk = sem("in_chunk")
        q_stacked = sem("q_stacked")
        k_stacked = [sem(f"k_stacked{i}") for i in range(3)]
        eps_set = sem("eps_set")
        const_set = sem("const_set")
        ones_set = sem("ones_set")
        w_hi_set, w_lo_set = sem("w_hi_set"), sem("w_lo_set")
        ln_stat, ln_std, ln_out, ln_t, ln_tc = sem("ln_stat"), sem("ln_std"), sem("ln_out"), sem("ln_t"), sem("ln_tc")
        q_mm, q_out = sem("q_mm"), sem("q_out")
        q_hi_set, q_lo_set = sem("q_hi_set"), sem("q_lo_set")
        c_hi_set, c_lo_set = sem("c_hi_set"), sem("c_lo_set")
        unit_mm = sem("unit_mm")
        unit_hi = sem("unit_hi")
        unit_lo = sem("unit_lo")
        v_mid, v_low = sem("v_mid"), sem("v_low")
        s_mm, s_max = sem("s_mm"), sem("s_max")
        m_red, m_hi, m_lo, m_mm, m_row = sem("m_red"), sem("m_hi"), sem("m_lo"), sem("m_mm"), sem("m_row")
        st_mm, p_exp, p_low, pv_mm = sem("st_mm"), sem("p_exp"), sem("p_low"), sem("pv_mm")
        a_out, dve_chain = sem("a_out"), sem("dve_chain")

        def unit_no(b, c, u):
            return (b * NCH + c) * UNITS + u

        def v_units(n):
            return n // UNITS * TT + min(n % UNITS, TT)

        def k_units(n):
            return n - v_units(n)

        T = {n: sem("t_" + n) for n in (
            "in_w0 in_w1 in_w2 in_w3 in_w4 in_w5 in_w6 in_x in_rows in_mask xo a a_tr a_tc y x1 std ln xn tr tc qkv mx sub "
            "exp v_sb v_st v_ld soft qt_mm q_tc k_tc g_mm g_m o_mm og o_st o_ld x2 std2 xn2 tr2 zero xp prev mix_k mix_r k_mm r_mm "
            "relu ka gate f_mm f_mul fin out chain pool om").split()}

        block = ctx.enter_context(nc.Block())
        NU = B * NCH * UNITS

        @block.sync
        def _(sp):
            sp.dma_start(x_in[:, :, :], x.rearrange("(b p) d -> p b d", p=P)).then_inc(in_x, 16)
            sp.dma_start(colt[:, :, :], cols).then_inc(in_small, 16)
            sp.dma_start(id32[:, :], ident).then_inc(in_small, 16)
            sp.dma_start(wq_sb[:, :, :], wq).then_inc(in_wq, 16)
            sp.dma_start(w_raw[:, 1, :, :], wv).then_inc(in_wv, 16)

            def load_chunk(n):
                if n:
                    sp.wait_ge(c_hi_set, n)
                    sp.wait_ge(c_lo_set, n)
                if n == NCH:
                    sp.wait_ge(pv_mm, 2 * H)
                sp.dma_start(c_raw[:, :, :], ctx_t[n]).then_inc(in_chunk, 16)

            load_chunk(0)
            sp.dma_start(w_raw[:, 0, :, :], wk).then_inc(in_wk, 16)
            for b in range(B):
                for c in range(NCH):
                    if b or c:
                        load_chunk(b * NCH + c)
                    if c == 0:
                        sp.wait_ge(q_hi_set, b + 1)
                        sp.wait_ge(q_lo_set, b + 1)
                        for j in range(HPT):
                            for r, part in enumerate((q_hi, q_hi, q_lo)):
                                dst = q_stack[HD * r:HD * r + HD, :, :].rearrange("p (m j) q -> p m j q", j=HPT)[:, :, j, :]
                                src = part[HD * j:HD * j + HD, :].rearrange("p (m q) -> p m q", m=MT)
                                sp.dma_start(dst.bitcast(F32), src.bitcast(F32)).then_inc(q_stacked, 16)
                n = (b + 1) * NCH * UNITS
                sp.wait_ge(unit_mm, n)
                sp.wait_ge(unit_hi, n)
                sp.wait_ge(unit_lo, n)
                sp.wait_ge(q_stacked, 16 * 12 * (b + 1))
                for h in range(H):
                    g, m, j = b * H + h, h // HPT, h % HPT
                    if h >= 3:
                        sp.wait_ge(st_mm, 2 * (g - 2))
                    for r, part in enumerate((k_hi, k_lo, k_hi)):
                        sp.dma_start(k_stack[HD * r:HD * r + HD, h % 3, :].bitcast(F32),
                                     part[HD * j:HD * j + HD, m, :].bitcast(F32)).then_inc(k_stacked[h % 3], 16)
                if b == B - 1:
                    sp.dma_start(x_res[:, :, :], x.rearrange("(b p) d -> p b d", p=P)).then_inc(T["in_x"], 16)
                    sp.dma_start(bias_rows[:, :, :], rows).then_inc(T["in_rows"], 16)
                    sp.dma_start(maskt[:, :, :], mask).then_inc(T["in_mask"], 16)
                    for i in range(3):
                        sp.wait_ge(k_stacked[i], 48 * sum(len(range(i, H, 3)) for _ in range(B)))
                    for i, (t, w) in enumerate(((wo_sb, wo), (w_q_sb, w_q), (w_k_sb, w_k), (w_v_sb, w_v),
                                                (f_k_sb, f_k), (f_r_sb, f_r), (f_v_sb, f_v))):
                        sp.dma_start(t[:, :, :], w).then_inc(T[f"in_w{i}"], 16)
            for t in range(B):
                sp.wait_ge(T["v_sb"], t + 1)
                sp.dma_start(v_dram[t], v_sb[:, t, :]).then_inc(T["v_st"], 16)
                sp.wait_ge(T["v_st"], 16 * (t + 1))
                sp.dma_start(vs[:, t, :, :], v_dram[t].rearrange("(g t) (h e) -> (t h) g e", t=TG, h=H)).then_inc(T["v_ld"], 16)
            for t in range(B):
                sp.wait_ge(T["og"], t + 1)
                sp.dma_start(o_dram[t].rearrange("(g t) (h e) -> (t h) g e", t=TG, h=H), og[:, t, :, :]).then_inc(T["o_st"], 16)
                sp.wait_ge(T["o_st"], 16 * (t + 1))
                sp.dma_start(o2[:, t, :], o_dram[t]).then_inc(T["o_ld"], 16)
            for t in range(B):
                sp.wait_ge(T["fin"], t + 1)
                sp.dma_start(out[t * LQ:(t + 1) * LQ, :], fin[:, t, :]).then_inc(T["out"], 16)
            sp.wait_ge(T["out"], 16 * B)

        @block.tensor
        def _(pe):
            pe.wait_ge(in_small, 32)
            for t in range(B):
                pe.wait_ge(ln_out, t + 1)
                for kt in range(KT):
                    last = pe.transpose(ps[:, 4 + t, kt * P:kt * P + P], xn0[:, t, kt * P:kt * P + P], id32[:, :])
                last.then_inc(ln_t, 1)
            pe.wait_ge(in_wq, 16)
            pe.wait_ge(ln_tc, B)
            for m in range(MT):
                o = ps[:, 4 + (m + 2) % 4, 0:B * LQ]
                for kt in range(KT):
                    last = pe.matmul(o, wq_sb[:, kt, m * P:m * P + P], xn0_t[:, kt, :, :].rearrange("p b q -> p (b q)"),
                                     start=kt == 0, stop=kt == KT - 1)
                last.then_inc(q_mm, 1)

            def project(b, c):
                pe.wait_ge(c_hi_set, b * NCH + c + 1)
                pe.wait_ge(c_lo_set, b * NCH + c + 1)
                s = c % 2
                for u in range(UNITS):
                    n = unit_no(b, c, u)
                    if n == 0:
                        pe.wait_ge(w_hi_set, 1)
                        pe.wait_ge(w_lo_set, 1)
                    if n == TT:
                        pe.wait_ge(w_hi_set, 2)
                        pe.wait_ge(w_lo_set, 2)
                    if n >= 4:
                        pe.wait_ge(unit_lo, n - 3)
                    o = ps[:, n % 4, :]
                    for i, (wh, xh) in enumerate(((0, 0), (0, 1), (1, 0))):
                        for kt in range(KT):
                            if u < TT:
                                lhs = (c_lo if xh else c_hi)[:, s, kt, u * P:u * P + P]
                                rhs = (wv_lo if wh else wv_hi)[:, kt, :]
                            else:
                                m = u - TT
                                lhs = (wk_lo if wh else wk_hi)[:, kt, m * P:m * P + P]
                                rhs = (c_lo if xh else c_hi)[:, s, kt, :]
                            last = pe.matmul(o, lhs, rhs, start=i == 0 and kt == 0, stop=i == 2 and kt == KT - 1)
                    last.then_inc(unit_mm, 1)

            def ring_free(b, s):
                s -= 2
                if s < 5 * H * b:
                    return
                g, i = divmod(s, 5)
                if i < 4:
                    pe.wait_ge(s_max, 4 * g + i + 1)
                else:
                    pe.wait_ge(m_row, g + 1)

            def scores(b, h):
                g = b * H + h
                pe.wait_ge(k_stacked[h % 3], 48 * (b * len(range(h % 3, H, 3)) + h // 3 + 1))
                for i in range(4):
                    s = 5 * g + i
                    ring_free(b, s)
                    pe.matmul(ps[:, s % 2, :], q_stack[0:SR, h, :], k_stack[0:SR, h % 3, i * CH:(i + 1) * CH],
                              start=True, stop=True).then_inc(s_mm, 1)

            def max_row(b, h):
                g = b * H + h
                s = 5 * g + 4
                pe.wait_ge(m_lo, g + 1)
                ring_free(b, s)
                pe.matmul(ps[:, s % 2, 0:P], m_cols[:, g % 2, :], id_r[:, :], start=True, stop=True).then_inc(m_mm, 1)

            def scores_t(b, h):
                g = b * H + h
                pe.wait_ge(m_row, g + 1)
                for i in range(2):
                    x_ = 2 * g + i
                    if x_ >= 2:
                        pe.wait_ge(p_exp, 2 * (x_ - 1))
                    for k in range(HALF):
                        kt = i * HALF + k
                        last = pe.matmul(ps[:, 2 + 2 * (x_ % 2) + k // 4, (k % 4) * LQ:(k % 4) * LQ + LQ],
                                         k_stack[0:SM, h % 3, kt * P:kt * P + P], q_stack[0:SM, h, :],
                                         start=True, stop=True)
                    last.then_inc(st_mm, 1)

            def weighted(b, h):
                g = b * H + h
                if g % HPT == 0 and g // HPT >= 2:
                    pe.wait_ge(a_out, g // HPT - 1)
                col = (h % HPT) * VC
                bank = 6 + (g // HPT) % 2
                for i in range(2):
                    x_ = 2 * g + i
                    pe.wait_ge(p_low, x_ + 1)
                    for k in range(HALF):
                        kt = i * HALF + k
                        pe.matmul(ps[:, bank, col:col + VC], p_hi[:, x_ % 3, k * LQ:k * LQ + LQ],
                                  v_parts[:, kt, h, :], start=kt == 0, stop=False)
                        last = pe.matmul(ps[:, bank, col + HD:col + VC], p_lo[:, x_ % 3, k * LQ:k * LQ + LQ],
                                         v_parts[:, kt, h, HD:VC], start=False, stop=kt == NKT - 1)
                    last.then_inc(pv_mm, 1)

            for b in range(B):
                for c in range(NCH):
                    project(b, c)
                pe.wait_ge(q_stacked, 16 * 12 * (b + 1))
                pe.wait_ge(unit_lo, (b + 1) * NCH * UNITS)
                pe.wait_ge(v_low, (b + 1) * NCH * TT)
                pe.wait_ge(ones_set, b + 1)
                scores(b, 0)
                max_row(b, 0)
                for h in range(H):
                    if h + 1 < H:
                        scores(b, h + 1)
                    scores_t(b, h)
                    if h:
                        weighted(b, h - 1)
                    if h + 1 < H:
                        max_row(b, h + 1)
                weighted(b, H - 1)

            def gemm(o, lhs, rhs):
                for kt in range(KT):
                    last = pe.matmul(o, lhs(kt), rhs(kt), start=kt == 0, stop=kt == KT - 1)
                return last

            def transposes(t, src, done):
                for kt in range(KT):
                    last = pe.transpose(ps[:, t, kt * P:kt * P + P], src[:, t, kt * P:kt * P + P], id32[:, :])
                last.then_inc(done, 1)

            pe.wait_ge(m_row, B * H)
            for t in range(B):
                pe.wait_ge(T["a"], t + 1)
                transposes(t, a_t, T["a_tr"])
            pe.wait_ge(T["in_w0"], 16)
            for t in range(B):
                pe.wait_ge(T["a_tc"], t + 1)
                gemm(ps[:, 2 + t, :], lambda kt: a_tt[:, t, kt, :], lambda kt: wo_sb[:, kt, :]).then_inc(T["y"], 1)
            for t in range(B):
                pe.wait_ge(T["xn"], t + 1)
                transposes(t, xn1, T["tr"])
            pe.wait_ge(T["tc"], B)
            for t in range(B):
                for i, w in enumerate((w_v_sb, w_k_sb, w_q_sb)):
                    pe.wait_ge(T[f"in_w{3 - i}"], 16)
                    gemm(ps[:, (4 + 3 * t + i) % 8, :], lambda kt: xn1_t[:, t, kt, :], lambda kt: w[:, kt, :]).then_inc(T["qkv"], 1)
            for t in range(B):
                pe.wait_ge(T["soft"], 2 * t + 2)
                for i in range(4):
                    n = 4 * t + i
                    for src, bank, freed in ((sq, 2, T["q_tc"]), (sk, 3, T["k_tc"])):
                        if n:
                            pe.wait_ge(freed, n)
                        for j in range(4):
                            h = 4 * i + j
                            last = pe.transpose(ps[0:HD, bank, j * P:j * P + P], src[:, t, h * HD:h * HD + HD], id32[:, :])
                        last.then_inc(T["qt_mm"], 1)
                pe.wait_ge(T["q_tc"], 4 * t + 4)
                pe.wait_ge(T["k_tc"], 4 * t + 4)
                if t == 0:
                    pe.wait_ge(T["sub"], 2)
                for i in range(NG // 4):
                    n = t * (NG // 4) + i
                    if n >= 2:
                        pe.wait_ge(T["g_m"], n - 1)
                    for j in range(4):
                        g = 4 * i + j
                        last = pe.matmul(ps[:, 5 + n % 2, j * P:j * P + P],
                                         k_t[:, t, g * TG:(g + 1) * TG, :].rearrange("p t h -> p (t h)"),
                                         q_t[:, t, g * TG:(g + 1) * TG, :].rearrange("p t h -> p (t h)"),
                                         start=True, stop=True)
                    last.then_inc(T["g_mm"], 1)
                pe.wait_ge(T["v_ld"], 16 * (t + 1))
                pe.wait_ge(T["g_m"], (t + 1) * (NG // 4))
                if t == 0:
                    pe.wait_ge(T["v_sb"], 2)
                for g in range(NG):
                    last = pe.matmul(ps[:, (4, 7)[t], g * HD:(g + 1) * HD], g_m[:, t, g, :], vs[:, t, g, :], start=True, stop=True)
                last.then_inc(T["o_mm"], 1)
            for t in range(B):
                pe.wait_ge(T["xn2"], t + 1)
                transposes(t, xn2, T["tr2"])
            pe.wait_ge(T["in_w4"], 16)
            for m in range(MT):
                if m == 0:
                    pe.wait_ge(T["mix_k"], KT)
                gemm(ps[:, 2 + m, 0:B * LQ], lambda kt: f_k_sb[:, kt, m * P:m * P + P],
                     lambda kt: xk[:, kt, :, :].rearrange("p b q -> p (b q)")).then_inc(T["k_mm"], 1)
            pe.wait_ge(T["in_w5"], 16)
            pe.wait_ge(T["mix_r"], KT)
            for t in range(B):
                gemm(ps[:, 6 + t, :], lambda kt: xr[:, kt, t, :], lambda kt: f_r_sb[:, kt, :]).then_inc(T["r_mm"], 1)
            pe.wait_ge(T["in_w6"], 16)
            pe.wait_ge(T["ka"], MT)
            for t in range(B):
                gemm(ps[:, t, :], lambda kt: ka[:, kt, t, :], lambda kt: f_v_sb[:, kt, :]).then_inc(T["f_mm"], 1)

        @block.scalar
        def _(act):
            act.wait_ge(eps_set, 1)
            for t in range(B):
                act.wait_ge(ln_stat, t + 1)
                act.activation(std[:, t:t + 1], mv[:, t, 1:2], ACT.Sqrt, bias=eps[:, :]).then_inc(ln_std, 1)
            for t in range(B):
                act.wait_ge(ln_t, t + 1)
                act.activation(xn0_t[:, :, t, :], ps[:, 4 + t, :].rearrange("p (k q) -> p k q", k=KT), ACT.Copy).then_inc(ln_tc, 1)
            act.wait_ge(in_wv, 16)
            act.activation(wv_hi[:, :, :], w_raw[:, 1, :, :], ACT.Copy).then_inc(w_hi_set, 1)

            def chunk_hi(n):
                act.wait_ge(in_chunk, 16 * (n + 1))
                if n % NCH >= 2:
                    act.wait_ge(unit_mm, (n - 1) * UNITS)
                act.activation(c_hi[:, n % 2, :, :], c_raw[:, :, :], ACT.Copy).then_inc(c_hi_set, 1)

            chunk_hi(0)
            act.wait_ge(in_wk, 16)
            act.activation(wk_hi[:, :, :], w_raw[:, 0, :, :], ACT.Copy).then_inc(w_hi_set, 1)
            for m in range(MT):
                act.wait_ge(q_mm, m + 1)
                act.activation(qa[:, :, m * P:m * P + P],
                               ps[:, 4 + (m + 2) % 4, 0:B * LQ].rearrange("p (b q) -> p b q", b=B),
                               ACT.Identity, bias=colt[:, 0, m:m + 1]).then_inc(q_out, 1)

            def exps(g, i):
                x_ = 2 * g + i
                act.wait_ge(st_mm, x_ + 1)
                if x_ >= 2:
                    act.wait_ge(p_low, x_ - 1)
                src = ps[:, 2 + 2 * (x_ % 2):4 + 2 * (x_ % 2), :].rearrange("p b c -> p (b c)")
                if x_ >= 3:
                    act.wait_ge(pv_mm, x_ - 2)
                act.activation(p_hi[:, x_ % 3, :], src, ACT.Exp, scale=SCALE).then_inc(p_exp, 1)
                act.activation(p_full[:, x_ % 2, :], src, ACT.Exp, scale=SCALE).then_inc(p_exp, 1)

            def max_row(b, h):
                g = b * H + h
                act.wait_ge(m_mm, g + 1)
                act.activation(q_stack[SR:SM, h, :], ps[SR:SM, (5 * g + 4) % 2, 0:LQ], ACT.Copy).then_inc(m_row, 1)

            for b in range(B):
                act.wait_ge(q_out, MT)
                if b:
                    act.wait_ge(pv_mm, 2 * H * b)
                act.activation(q_hi[:, :], qa[:, b, :], ACT.Copy).then_inc(q_hi_set, 1)
                for c in range(NCH):
                    if c == 0 and b:
                        chunk_hi(b * NCH)
                    if c + 1 < NCH:
                        chunk_hi(b * NCH + c + 1)
                    for u in range(UNITS):
                        n = unit_no(b, c, u)
                        act.wait_ge(unit_mm, n + 1)
                        if u < TT:
                            if n == 0:
                                act.wait_ge(w_lo_set, 2)
                                act.wait_ge(const_set, 1)
                                act.wait_ge(q_mm, MT)
                            act.activation(v_parts[:, c * TT + u, :, HD:2 * HD],
                                           ps[:, n % 4, :].rearrange("p (h e) -> p h e", h=H), ACT.Copy).then_inc(unit_hi, 1)
                        else:
                            m = u - TT
                            act.activation(k_hi[:, m, c * CH:(c + 1) * CH], ps[:, n % 4, :], ACT.Identity,
                                           bias=colt[:, 1, m:m + 1]).then_inc(unit_hi, 1)
                max_row(b, 0)
                for h in range(H):
                    exps(b * H + h, 0)
                    if h + 1 < H:
                        max_row(b, h + 1)
                    exps(b * H + h, 1)

            for t in range(B):
                act.wait_ge(T["a_tr"], t + 1)
                act.activation(a_tt[:, t, :, :].rearrange("p k q -> p (k q)"), ps[:, t, :], ACT.Copy).then_inc(T["a_tc"], 1)
            for t in range(B):
                act.wait_ge(T["ln"], t + 1)
                act.activation(std[:, t:t + 1], mv[:, t, 1:2], ACT.Sqrt, bias=eps[:, :]).then_inc(T["std"], 1)
            for t in range(B):
                act.wait_ge(T["tr"], t + 1)
                act.activation(xn1_t[:, t, :, :].rearrange("p k q -> p (k q)"), ps[:, t, :], ACT.Copy).then_inc(T["tc"], 1)
            for t in range(B):
                act.wait_ge(T["qkv"], 3 * t + 1)
                act.activation(v_sb[:, t, :], ps[:, 4 + 3 * t, :], ACT.Copy).then_inc(T["v_sb"], 1)
                for i, s_ in enumerate((sk, sq)):
                    act.wait_ge(T["sub"], 2 * t + i + 1)
                    act.activation(s_[:, t, :], s_[:, t, :], ACT.Exp).then_inc(T["exp"], 1)
            for t in range(B):
                for i in range(4):
                    act.wait_ge(T["qt_mm"], 8 * t + 2 * i + 1)
                    act.activation(q_t[:, t, :, 4 * i:4 * i + 4].rearrange("p q h -> p h q"),
                                   ps[0:HD, 2, :].rearrange("p (h q) -> p h q", h=4), ACT.Copy).then_inc(T["q_tc"], 1)
                act.wait_ge(T["o_mm"], t + 1)
                act.activation(og[:, t, :, :].rearrange("p g e -> p (g e)"), ps[:, (4, 7)[t], :], ACT.Copy).then_inc(T["og"], 1)
            for t in range(B):
                act.wait_ge(T["x2"], 2 * t + 2)
                act.activation(std[:, t:t + 1], mv[:, t, 1:2], ACT.Sqrt, bias=eps[:, :]).then_inc(T["std2"], 1)
            act.wait_ge(T["zero"], 1)
            for t in range(B):
                act.wait_ge(T["tr2"], t + 1)
                act.activation(xp_t[:, :, t, 1:LQ + 1], ps[:, t, :].rearrange("p (k q) -> p k q", k=KT), ACT.Copy).then_inc(T["xp"], 1)
            act.wait_ge(T["xp"], B)
            act.wait_ge(T["om"], 1)
            for i in (1, 0):
                for kt in range(KT):
                    act.activation(prev[:, i, kt, :, :], xp_t[:, kt, :, 0:LQ], ACT.Copy, scale=om[:, i, kt:kt + 1]).then_inc(T["prev"], 1)
            for m in range(MT):
                act.wait_ge(T["k_mm"], m + 1)
                act.activation(relu[:, m, :, :].rearrange("p b q -> p (b q)"), ps[:, 2 + m, 0:B * LQ], ACT.Relu).then_inc(T["relu"], 1)
            for t in range(B):
                act.wait_ge(T["r_mm"], t + 1)
                act.activation(gate[:, t, :], ps[:, 6 + t, :], ACT.Sigmoid).then_inc(T["gate"], 1)

        @block.vector
        def _(dve):
            chain = [0]

            def link(ins):
                chain[0] += 1
                ins.then_inc(dve_chain, 1)
                dve.wait_ge(dve_chain, chain[0])

            dve.memset(eps[:, :], EPS).then_inc(eps_set, 1)
            dve.wait_ge(in_x, 16)
            for t in range(B):
                link(dve.bn_stats(stat[:, t, :], x_in[:, t, :]))
                dve.bn_aggr(mv[:, t, :], stat[:, t, :]).then_inc(ln_stat, 1)
            dve.wait_ge(ln_stat, B)
            for t in range(B):
                dve.wait_ge(ln_std, t + 1)
                link(dve.reciprocal(rstd[:, t:t + 1], std[:, t:t + 1]))
                dve.tensor_scalar(xn0[:, t, :], x_in[:, t, :], mv[:, t, 0:1], rstd[:, t:t + 1],
                                  ALU.subtract, ALU.mult).then_inc(ln_out, 1)
            dve.wait_ge(in_small, 32)
            link(dve.tensor_copy(id_r[:, :], id32[:, :]))
            dve.wait_ge(w_hi_set, 1)
            dve.tensor_tensor(wv_lo[:, :, :], w_raw[:, 1, :, :], wv_hi[:, :, :].bitcast(F32), ALU.subtract).then_inc(w_lo_set, 1)

            def chunk_lo(n):
                dve.wait_ge(c_hi_set, n + 1)
                dve.tensor_tensor(c_lo[:, n % 2, :, :], c_raw[:, :, :], c_hi[:, n % 2, :, :].bitcast(F32),
                                  ALU.subtract).then_inc(c_lo_set, 1)

            chunk_lo(0)
            dve.wait_ge(w_hi_set, 2)
            dve.tensor_tensor(wk_lo[:, :, :], w_raw[:, 0, :, :], wk_hi[:, :, :].bitcast(F32), ALU.subtract).then_inc(w_lo_set, 1)

            def maximum(b, h):
                g = b * H + h
                if g:
                    dve.wait_ge(m_red, g)
                for i in range(4):
                    dve.wait_ge(s_mm, 4 * g + i + 1)
                    dve.tensor_reduce(pm[:, i:i + 1], ps[:, (5 * g + i) % 2, :], AX_X, ALU.max).then_inc(s_max, 1)
                dve.wait_ge(s_max, 4 * g + 4)
                if g:
                    dve.wait_ge(m_lo, g)
                dve.tensor_reduce(m_q[:, :], pm[:, :], AX_X, ALU.max).then_inc(m_red, 1)
                dve.wait_ge(m_red, g + 1)
                if g >= 2:
                    dve.wait_ge(m_mm, g - 1)
                dve.tensor_scalar(m_cols[:, g % 2, SR:SR + 1], m_q[:, :], -1.0, LIFT, ALU.mult, ALU.add).then_inc(m_hi, 1)
                dve.tensor_scalar(pm[:, 0:1], m_q[:, :], -1.0, LIFT, ALU.mult, ALU.add).then_inc(m_hi, 1)
                dve.wait_ge(m_hi, 2 * g + 2)
                dve.tensor_tensor(m_cols[:, g % 2, SR + 1:SR + 2], pm[:, 0:1],
                                  m_cols[:, g % 2, SR:SR + 1].bitcast(F32), ALU.subtract).then_inc(m_lo, 1)

            def lows(g, i):
                x_ = 2 * g + i
                dve.wait_ge(p_exp, 2 * (x_ + 1))
                if x_ >= 3:
                    dve.wait_ge(pv_mm, x_ - 2)
                dve.tensor_tensor(p_lo[:, x_ % 3, :], p_full[:, x_ % 2, :], p_hi[:, x_ % 3, :], ALU.subtract).then_inc(p_low, 1)

            def gather(b, m):
                k = b * MT + m
                dve.wait_ge(pv_mm, 2 * HPT * (k + 1))
                acc = ps[:, 6 + k % 2, 0:HPT * VC].rearrange("p (j c) -> p j c", j=HPT)
                dst = qa[:, b, m * P:m * P + P].rearrange("p (j e) -> p j e", j=HPT)
                link(dve.tensor_reduce(dst, acc[:, :, 0:3 * HD].rearrange("p j (c e) -> p j e c", c=3), AX_X, ALU.add))
                link(dve.reciprocal(rec[:, :], acc[:, :, VC - 1]))
                for j in range(HPT):
                    last = dve.tensor_scalar(dst[:, j, :], dst[:, j, :], rec[:, j:j + 1], None, ALU.mult)
                last.then_inc(a_out, 1)
                dve.wait_ge(a_out, k + 1)

            for b in range(B):
                dve.wait_ge(q_hi_set, b + 1)
                dve.tensor_tensor(q_lo[:, :], qa[:, b, :], q_hi[:, :].bitcast(F32), ALU.subtract).then_inc(q_lo_set, 1)
                for c in range(NCH):
                    if c == 0 and b:
                        chunk_lo(b * NCH)
                    if c + 1 < NCH:
                        chunk_lo(b * NCH + c + 1)
                    for u in range(UNITS):
                        n = unit_no(b, c, u)
                        dve.wait_ge(unit_hi, n + 1)
                        if u < TT:
                            v = v_units(n)
                            if v >= 2:
                                dve.wait_ge(v_low, v - 1)
                            dve.tensor_tensor(r1[:, v % 2, :].rearrange("p (h e) -> p h e", h=H),
                                              ps[:, n % 4, :].rearrange("p (h e) -> p h e", h=H),
                                              v_parts[:, c * TT + u, :, HD:2 * HD], ALU.subtract).then_inc(unit_lo, 1)
                        else:
                            m = u - TT
                            dve.scalar_tensor_tensor(k_lo[:, m, c * CH:(c + 1) * CH], ps[:, n % 4, :], colt[:, 1, m:m + 1],
                                                     k_hi[:, m, c * CH:(c + 1) * CH].bitcast(F32),
                                                     ALU.add, ALU.subtract).then_inc(unit_lo, 1)
                if b == 0:
                    dve.wait_ge(const_set, 2)
                maximum(b, 0)
                for h in range(H):
                    if h + 1 < H:
                        maximum(b, h + 1)
                    if h >= 5 and (h - 5) % HPT == 0:
                        gather(b, (h - 5) // HPT)
                    lows(b * H + h, 0)
                    lows(b * H + h, 1)
                gather(b, MT - 1)

            dve.wait_ge(T["in_rows"], 16)
            for t in range(B):
                dve.tensor_tensor(a_t[:, t, :], qa[:, t, :], bias_rows[:, 0, :], ALU.add).then_inc(T["a"], 1)

            def layernorm(t, src, dst, stat_done, std_done, out_done):
                link(dve.bn_stats(stat[:, t, :], src[:, t, :]))
                dve.bn_aggr(mv[:, t, :], stat[:, t, :]).then_inc(stat_done, 1)

            def normalise(t, src, dst, std_done, out_done):
                dve.wait_ge(std_done, t + 1)
                link(dve.reciprocal(rstd[:, t:t + 1], std[:, t:t + 1]))
                dve.tensor_scalar(dst[:, t, :], src[:, t, :], mv[:, t, 0:1], rstd[:, t:t + 1],
                                  ALU.subtract, ALU.mult).then_inc(out_done, 1)

            dve.wait_ge(T["xo"], 2)
            for t in range(B):
                dve.wait_ge(T["y"], t + 1)
                link(dve.tensor_tensor(x1[:, t, :], ps[:, 2 + t, :], xo[:, t, :], ALU.add))
                layernorm(t, x1, xn1, T["ln"], None, None)
            dve.wait_ge(T["ln"], B)
            for t in range(B):
                normalise(t, x1, xn1, T["std"], T["xn"])

            def groups(t, i):
                bank = (4 + 3 * t + 1 + i) % 8
                s_ = (sk, sq)[i]
                if i == 0:
                    v = lambda a: a.rearrange("p (h e) -> p e h", h=H)
                    lo, hi = 0, HD
                else:
                    v = lambda a: a.rearrange("p (h e) -> p h e", h=H)
                    lo, hi = HD, HD + H
                return v(ps[:, bank, :]), v(s_[:, t, :]), slice(lo, hi)

            def spread(a, n):
                return a.unsqueeze(2).to_broadcast([P, a.shape[1], n])

            dve.wait_ge(m_mm, B * H)
            for t in range(B):
                for i in range(2):
                    dve.wait_ge(T["qkv"], 3 * t + i + 2)
                    src, dst, c = groups(t, i)
                    link(dve.tensor_reduce(mx[:, t, c], src, AX_X, ALU.max))
                    dve.tensor_tensor(dst, src, spread(mx[:, t, c], src.shape[2]), ALU.subtract).then_inc(T["sub"], 1)
            for t in range(B):
                for i in range(2):
                    dve.wait_ge(T["exp"], 2 * t + i + 1)
                    src, dst, c = groups(t, i)
                    link(dve.tensor_reduce(sm[:, t, c], dst, AX_X, ALU.add))
                    link(dve.reciprocal(rs[:, t, c], sm[:, t, c]))
                    dve.tensor_tensor(dst, dst, spread(rs[:, t, c], dst.shape[2]), ALU.mult).then_inc(T["soft"], 1)
            dve.wait_ge(T["in_mask"], 16)
            for t in range(B):
                for i in range(4):
                    dve.wait_ge(T["qt_mm"], 8 * t + 2 * i + 2)
                    dve.tensor_copy(k_t[:, t, :, 4 * i:4 * i + 4].rearrange("p q h -> p h q"),
                                    ps[0:HD, 3, :].rearrange("p (h q) -> p h q", h=4)).then_inc(T["k_tc"], 1)
                for i in range(NG // 4):
                    n = t * (NG // 4) + i
                    dve.wait_ge(T["g_mm"], n + 1)
                    dve.tensor_tensor(g_m[:, t, 4 * i:4 * i + 4, :].rearrange("p g c -> p (g c)"), ps[:, 5 + n % 2, :],
                                      maskt[:, :, :].rearrange("p g c -> p (g c)"), ALU.mult).then_inc(T["g_m"], 1)
            for t in range(B):
                dve.wait_ge(T["o_ld"], 16 * (t + 1))
                dve.tensor_tensor(x2[:, t, :], x1[:, t, :], o2[:, t, :], ALU.add).then_inc(T["x2"], 1)
                dve.wait_ge(T["x2"], 2 * t + 1)
                layernorm(t, x2, xn2, T["x2"], None, None)
            dve.wait_ge(T["x2"], 2 * B)
            for t in range(B):
                normalise(t, x2, xn2, T["std2"], T["xn2"])
            dve.wait_ge(T["xp"], B)
            dve.wait_ge(T["o_mm"], B)
            for n, (i, dst, done) in enumerate(((1, xk, T["mix_k"]), (0, xr, T["mix_r"]))):
                for kt in range(KT):
                    dve.wait_ge(T["prev"], n * KT + kt + 1)
                    dve.scalar_tensor_tensor(dst[:, kt, :, :], xp_t[:, kt, :, 1:LQ + 1], colt[:, 2 + i, kt:kt + 1],
                                             prev[:, i, kt, :, :], ALU.mult, ALU.add).then_inc(done, 1)
            for m in range(MT):
                dve.wait_ge(T["relu"], m + 1)
                dve.tensor_tensor(ka[:, m, :, :], relu[:, m, :, :], relu[:, m, :, :], ALU.mult).then_inc(T["ka"], 1)
            for t in range(B):
                dve.wait_ge(T["gate"], t + 1)
                dve.wait_ge(T["f_mm"], t + 1)
                link(dve.tensor_tensor(fin[:, t, :], ps[:, t, :], gate[:, t, :], ALU.mult))
                dve.tensor_tensor(fin[:, t, :], fin[:, t, :], x2[:, t, :], ALU.add).then_inc(T["fin"], 1)

        @block.gpsimd
        def _(pool):
            pool.wait_ge(w_lo_set, 2)
            pool.wait_ge(q_mm, MT)
            pool.memset(v_parts[:, :, :, VC - 1], 1.0).then_inc(const_set, 1)
            pool.memset(m_cols[:, :, :].bitcast(F32), 0.0).then_inc(const_set, 1)
            pool.wait_ge(in_small, 32)
            pool.tensor_scalar(om[:, :, :], colt[:, 2:4, :], -1.0, 1.0, ALU.mult, ALU.add).then_inc(T["om"], 1)
            for b in range(B):
                for c in range(NCH):
                    for u in range(TT):
                        n = unit_no(b, c, u)
                        v = v_units(n)
                        tile = v_parts[:, c * TT + u]
                        rest = r1[:, v % 2, :].rearrange("p (h e) -> p h e", h=H)
                        pool.wait_ge(unit_lo, n + 1)
                        pool.tensor_copy(tile[:, :, 2 * HD:3 * HD], rest).then_inc(v_mid, 1)
                        pool.wait_ge(v_mid, v + 1)
                        pool.tensor_tensor(tile[:, :, 0:HD], rest, tile[:, :, 2 * HD:3 * HD], ALU.subtract).then_inc(v_low, 1)
                pool.wait_ge(unit_mm, (b + 1) * NCH * UNITS)
                pool.wait_ge(v_low, (b + 1) * NCH * TT)
                pool.memset(k_stack[SR:SM, :, :].bitcast(F32), 1.0).then_inc(ones_set, 1)
            pool.wait_ge(T["in_x"], 16)
            pool.wait_ge(T["in_rows"], 16)
            for t in range(B):
                pool.tensor_tensor(xo[:, t, :], x_res[:, t, :], bias_rows[:, 1, :], ALU.add).then_inc(T["xo"], 1)
            pool.wait_ge(pv_mm, 2 * B * H)
            pool.memset(xp_t[:, :, :, 0:1], 0.0).then_inc(T["zero"], 1)


def kernel(**inputs):
    import numpy as np
    import concourse.bacc as bacc
    from concourse.bass_utils import run_bass_kernel_spmd

    a = {k: np.asarray(v) for k, v in inputs.items()}

    def tiles(w):
        return np.ascontiguousarray(w.reshape(KT, P, D).transpose(1, 0, 2))

    def col(v):
        return v.reshape(KT, P).T

    ctx_in = a["ctx_1024"].reshape(B * NCH, CH, KT, P).transpose(0, 3, 2, 1)
    block = np.kron(np.eye(TG, dtype=np.float32), np.ones((H, H), np.float32))
    data = {
        "x": a["x"].reshape(B * LQ, D),
        "ctx_t": ctx_in,
        "wq": tiles(a["L0_xattn_Wq"]), "wk": tiles(a["L0_xattn_Wk"]), "wv": tiles(a["L0_xattn_Wv"]),
        "wo": tiles(a["L0_xattn_Wo"]),
        "w_q": tiles(a["L0_attn_W_Q"].T), "w_k": tiles(a["L0_attn_W_K"].T), "w_v": tiles(a["L0_attn_W_V"].T),
        "f_r": tiles(a["L0_ffn_W_r"].T), "f_k": tiles(a["L0_ffn_W_k"].T), "f_v": tiles(a["L0_ffn_W_v"].T),
        "cols": np.stack([col(a["L0_xattn_bq"]), col(a["L0_xattn_bk"]), col(a["L0_ffn_mu_r"]), col(a["L0_ffn_mu_k"])], 1),
        "rows": np.broadcast_to(np.stack([a["L0_xattn_bv"], a["L0_xattn_bo"]])[None], (P, 2, D)),
        "ident": np.eye(P, dtype=np.float32),
        "mask": np.broadcast_to(block[:, None, :], (P, 4, P)),
    }
    nc = bacc.Bacc("TRN2", target_bir_lowering=False, num_devices=1)
    arrays, args = {}, []
    for name, v in data.items():
        v = np.ascontiguousarray(v)
        arrays[f"in_{name}"] = v
        args.append(nc.dram_tensor(f"in_{name}", v.shape, F32, kind="ExternalInput").ap())
    out = nc.dram_tensor("out", [B * LQ, D], F32, kind="ExternalOutput").ap()
    perceiver(nc, *args, out)
    r = run_bass_kernel_spmd(nc, [arrays], core_ids=[0])
    return r.results[0]["out"].reshape(B, LQ, D)
```

```python
from contextlib import ExitStack

import concourse.bass as bass
from concourse import mybir

F32 = mybir.dt.float32
F32R = mybir.dt.float32r
BF16 = mybir.dt.bfloat16
F16 = mybir.dt.float16
ALU = mybir.AluOpType
ACT = mybir.ActivationFunctionType
AX_X = mybir.AxisListType.X

P = 128
B = 2
LQ = 128
D = 512
KT = D // P
LK = 2048
H = 16
HD = D // H
MT = D // P
HPT = P // HD
CH = 512
NCH = LK // CH
TT = CH // P
NKT = LK // P
UNITS = MT + TT
UB = 2
NSLOT = 4
VC = 3 * HD + 1
SR = 3 * HD
HALF = NKT // 2
FH = HALF * LQ
TG = P // H
NG = LQ // TG
EPS = 1e-5
SCALE = 1.0 / HD ** 0.5
LIFT = 14 * 0.6931471805599453 / SCALE


def perceiver(nc, x, ctx_t, wq, wk, wv, wo, w_q, w_k, w_v, f_r, f_k, f_v, cols, rows, ident, mask, out):
    v_dram = nc.dram_tensor("v_rows", [B, LQ, D], F32, kind="Internal").ap()
    wk_lo_dram = nc.dram_tensor("wk_lo_kept", [P, KT * D], F32, kind="Internal").ap()
    o_dram = nc.dram_tensor("mixed_rows", [B, LQ, D], F32, kind="Internal").ap()

    with ExitStack() as ctx:
        def sem(name):
            return ctx.enter_context(nc.semaphore(name))

        base = (nc.sbuf_base + 31) // 32 * 32
        at = [base]

        def place(name, shape, dt, size=None):
            n = 1
            for s in shape[1:]:
                n *= s
            n *= 2 if dt in (BF16, F16) else 4
            t = nc.alloc_sbuf_tensor_at(name, shape, dt, offset=at[0])
            at[0] += (n + 31) // 32 * 32
            return t

        k_hi = place("k_hi", [P, MT, LK], F32R)
        k_lo = place("k_lo", [P, MT, LK], F32R)
        v_at = at[0]
        v_parts = place("v_parts", [P, NKT, H, VC], BF16)
        w_at = at[0]
        wk_hi = place("wk_hi", [P, KT, D], F32R)
        wk_lo_at = at[0]
        wk_lo = place("wk_lo", [P, KT, D], F32R)
        wv_hi = place("wv_hi", [P, KT, D], F32R)
        wv_lo = place("wv_lo", [P, KT, D], F32R)
        both_at = at[0]
        c_raw = place("c_raw", [P, KT, CH], F32)
        c_hi = place("c_hi", [P, 2, KT, CH], F32R)
        c_lo = place("c_lo", [P, 2, KT, CH], F32R)
        q_hi = place("q_hi", [P, D], F32R)
        q_lo = place("q_lo", [P, D], F32R)
        both_end = at[0]
        at[0] = both_at
        k_stack = place("k_stack", [P, 3, LK], F32R)
        p_full = place("p_full", [P, 2, FH], F32)
        p_hi = place("p_hi", [P, 3, FH], F16)
        p_lo = place("p_lo", [P, 3, FH], F16)
        assert at[0] <= both_end
        at[0] = wk_lo_at
        k_stack3 = place("k_stack3", [P, LK], F32R)
        at[0] = both_end
        q_stack = place("q_stack", [P, H, LQ], F32R)
        qa = place("qa", [P, B, D], F32)
        r1 = place("r1", [P, 2, D], F32)
        id32 = place("id32", [P, P], F32)
        id_r = place("id_r", [P, P], F32R)
        m_cols = place("m_cols", [P, 2, P], F32R)
        colt = place("colt", [P, 4, KT], F32)
        om = place("om", [P, 2, KT], F32)
        stat = place("stat", [P, 2, 6], F32)
        mv = place("mv", [P, 2, 2], F32)
        std = place("std", [P, 2], F32)
        rstd = place("rstd", [P, 2], F32)
        eps = place("eps", [P, 1], F32)
        pm = place("pm", [P, 4], F32)
        m_q = place("m_q", [P, 1], F32)
        rec = place("rec", [P, 4], F32)
        warm = place("warm", [P, 1], F32)
        assert at[0] <= nc.sbuf_top, (at[0], nc.sbuf_top)

        at[0] = v_at
        w_raw = place("w_raw", [P, 2, KT, D], F32)
        wq_sb = place("wq_sb", [P, KT, D], F32)
        x_in = place("x_in", [P, B, D], F32)
        xn0 = place("xn0", [P, B, D], F32)
        xn0_t = place("xn0_t", [P, KT, B, LQ], F32)
        assert at[0] <= w_at
        at[0] = base
        names = ["wo_sb", "w_q_sb", "w_k_sb", "w_v_sb", "f_k_sb", "f_r_sb", "f_v_sb"]
        wo_sb, w_q_sb, w_k_sb, w_v_sb, f_k_sb, f_r_sb, f_v_sb = [place(n, [P, KT, D], F32) for n in names]
        assert at[0] <= v_at
        at[0] = w_at
        x_res = place("x_res", [P, B, D], F32)
        bias_rows = place("bias_rows", [P, 2, D], F32)
        maskt = place("maskt", [P, 4, P], F32)
        xo = place("xo", [P, B, D], F32)
        a_t = place("a_t", [P, B, D], F32)
        x1 = place("x1", [P, B, D], F32)
        xn1 = place("xn1", [P, B, D], F32)
        xn1_t = place("xn1_t", [P, B, KT, LQ], F32)
        assert at[0] <= both_at
        vs = place("vs", [P, B, NG, HD], F32)
        og = place("og", [P, B, NG, HD], F32)
        o2 = place("o2", [P, B, D], F32)
        x2 = place("x2", [P, B, D], F32)
        xn2 = place("xn2", [P, B, D], F32)
        xp_t = place("xp_t", [P, KT, B, LQ + 1], F32)
        prev = place("prev", [P, 2, KT, B, LQ], F32)
        assert at[0] <= both_end
        at[0] = v_at
        g_m = place("g_m", [P, B, NG, P], F32)
        q_t = place("q_t", [HD, B, LQ, H], F32)
        k_t = place("k_t", [HD, B, LQ, H], F32)
        assert at[0] <= w_at
        at[0] = v_at
        xr = place("xr", [P, KT, B, LQ], F32)
        xk = place("xk", [P, KT, B, LQ], F32)
        relu = place("relu", [P, MT, B, LQ], F32)
        ka = place("ka", [P, MT, B, LQ], F32)
        assert at[0] <= v_at + 16384
        at[0] = both_end
        gate = place("gate", [P, B, D], F32)
        fin = place("fin", [P, B, D], F32)
        at[0] = base + 7 * 8192
        a_tt = place("a_tt", [P, B, KT, LQ], F32)
        v_sb = place("v_sb", [P, B, D], F32)
        assert at[0] <= v_at
        at[0] = both_end + 8192
        sq = place("sq", [P, B, D], F32)
        sk = place("sk", [P, B, D], F32)
        at[0] = both_end + 8192 + 8192 + 512
        mx = place("mx", [P, B, 48], F32)
        sm = place("sm", [P, B, 48], F32)
        rs = place("rs", [P, B, 48], F32)

        ps = ctx.enter_context(nc.psum_tensor("ps", [P, 8, 512], F32))

        in_x, in_wq, in_wk, in_wv = sem("in_x"), sem("in_wq"), sem("in_wk"), sem("in_wv")
        in_small = sem("in_small")
        in_chunk = sem("in_chunk")
        q_stacked = sem("q_stacked")
        k_stacked = [sem(f"k_stacked{i}") for i in range(NSLOT)]
        wk_lo_kept = sem("wk_lo_kept")
        wk_lo_back = sem("wk_lo_back")
        eps_set = sem("eps_set")
        const_set = sem("const_set")
        ones_set = sem("ones_set")
        zeros_set = sem("zeros_set")
        exp_loaded = sem("exp_loaded")
        w_hi_set, w_lo_set = sem("w_hi_set"), sem("w_lo_set")
        ln_stat, ln_std, ln_out, ln_t, ln_tc = sem("ln_stat"), sem("ln_std"), sem("ln_out"), sem("ln_t"), sem("ln_tc")
        q_mm, q_out = sem("q_mm"), sem("q_out")
        q_hi_set, q_lo_set = sem("q_hi_set"), sem("q_lo_set")
        c_hi_set, c_lo_set = sem("c_hi_set"), sem("c_lo_set")
        unit_mm = sem("unit_mm")
        unit_hi = sem("unit_hi")
        unit_lo = sem("unit_lo")
        v_mid, v_low = sem("v_mid"), sem("v_low")
        s_mm, s_max = sem("s_mm"), sem("s_max")
        m_red, m_hi, m_lo, m_mm, m_row = sem("m_red"), sem("m_hi"), sem("m_lo"), sem("m_mm"), sem("m_row")
        st_mm, p_exp, pv_mm = sem("st_mm"), sem("p_exp"), sem("pv_mm")
        p_low = [sem("p_low_first"), sem("p_low_second")]
        a_out, dve_chain = sem("a_out"), sem("dve_chain")

        def k_slot(h):
            return k_stack[:, h % NSLOT, :] if h % NSLOT < 3 else k_stack3[:, :]

        def unit_no(b, c, u):
            return (b * NCH + c) * UNITS + u

        def v_units(n):
            return n // UNITS * TT + max(n % UNITS - MT, 0)

        T = {n: sem("t_" + n) for n in (
            "in_w0 in_w1 in_w2 in_w3 in_w4 in_w5 in_w6 in_x in_rows in_mask xo a a_tr a_tc y x1 std ln xn tr tc qkv mx sub "
            "exp v_sb v_st v_ld soft qt_mm q_tc k_tc g_mm g_m o_mm og o_st o_ld x2 std2 xn2 tr2 zero xp prev mix_k mix_r k_mm r_mm "
            "relu ka gate f_mm f_mul fin out chain pool om").split()}

        block = ctx.enter_context(nc.Block())
        NU = B * NCH * UNITS

        @block.sync
        def _(sp):
            def load_chunk(n):
                if n:
                    sp.wait_ge(c_hi_set, n)
                    sp.wait_ge(c_lo_set, n)
                if n == NCH:
                    sp.wait_ge(st_mm, 2 * (H - NSLOT + 1))
                sp.dma_start(c_raw[:, :, :], ctx_t[n]).then_inc(in_chunk, 16)

            sp.dma_start(w_raw[:, 0, :, :], wk).then_inc(in_wk, 16)
            load_chunk(0)
            sp.dma_start(w_raw[:, 1, :, :], wv).then_inc(in_wv, 16)
            sp.dma_start(x_in[:, :, :], x.rearrange("(b p) d -> p b d", p=P)).then_inc(in_x, 16)
            sp.dma_start(colt[:, :, :], cols).then_inc(in_small, 16)
            sp.dma_start(id32[:, :], ident).then_inc(in_small, 16)
            sp.dma_start(wq_sb[:, :, :], wq).then_inc(in_wq, 16)

            for b in range(B):
                load_chunk(b * NCH + (b == 0))
                if b == 0:
                    sp.wait_ge(w_lo_set, 1)
                    sp.dma_start(wk_lo_dram, wk_lo[:, :, :].rearrange("p k n -> p (k n)").bitcast(F32)).then_inc(wk_lo_kept, 16)
                else:
                    sp.wait_ge(st_mm, 2 * H * b)
                    sp.wait_ge(wk_lo_kept, 16)
                    sp.dma_start(wk_lo[:, :, :].rearrange("p k n -> p (k n)").bitcast(F32), wk_lo_dram).then_inc(wk_lo_back, 16)
                    load_chunk(b * NCH + 1)
                sp.wait_ge(q_hi_set, b + 1)
                sp.wait_ge(q_lo_set, b + 1)
                for j in range(HPT):
                    for r, part in enumerate((q_hi, q_hi, q_lo)):
                        dst = q_stack[HD * r:HD * r + HD, :, :].rearrange("p (m j) q -> p m j q", j=HPT)[:, :, j, :]
                        src = part[HD * j:HD * j + HD, :].rearrange("p (m q) -> p m q", m=MT)
                        sp.dma_start(dst.bitcast(F32), src.bitcast(F32)).then_inc(q_stacked, 16)
                for c in range(2, NCH):
                    load_chunk(b * NCH + c)
                n = unit_no(b, NCH - 1, MT)
                sp.wait_ge(unit_hi, n)
                sp.wait_ge(unit_lo, n)
                sp.wait_ge(c_lo_set, (b + 1) * NCH)
                sp.wait_ge(wk_lo_kept, 16)
                for h in range(H):
                    g, m, j = b * H + h, h // HPT, h % HPT
                    if h == 2:
                        sp.wait_ge(unit_mm, (b + 1) * NCH * UNITS)
                    if h >= NSLOT:
                        sp.wait_ge(st_mm, 2 * (g - NSLOT + 1))
                    for r, part in enumerate((k_hi, k_lo, k_hi)):
                        sp.dma_start(k_slot(h)[HD * r:HD * r + HD, :].bitcast(F32),
                                     part[HD * j:HD * j + HD, m, :].bitcast(F32)).then_inc(k_stacked[h % NSLOT], 16)
                if b == B - 1:
                    sp.wait_ge(st_mm, 2 * B * H)
                    sp.dma_start(x_res[:, :, :], x.rearrange("(b p) d -> p b d", p=P)).then_inc(T["in_x"], 16)
                    sp.dma_start(bias_rows[:, :, :], rows).then_inc(T["in_rows"], 16)
                    sp.dma_start(maskt[:, :, :], mask).then_inc(T["in_mask"], 16)
                    for i in range(NSLOT):
                        sp.wait_ge(k_stacked[i], 48 * B * H // NSLOT)
                    for i, (t, w) in enumerate(((wo_sb, wo), (w_q_sb, w_q), (w_k_sb, w_k), (w_v_sb, w_v),
                                                (f_k_sb, f_k), (f_r_sb, f_r), (f_v_sb, f_v))):
                        sp.dma_start(t[:, :, :], w).then_inc(T[f"in_w{i}"], 16)
            for t in range(B):
                sp.wait_ge(T["v_sb"], t + 1)
                sp.dma_start(v_dram[t], v_sb[:, t, :]).then_inc(T["v_st"], 16)
                sp.wait_ge(T["v_st"], 16 * (t + 1))
                sp.dma_start(vs[:, t, :, :], v_dram[t].rearrange("(g t) (h e) -> (t h) g e", t=TG, h=H)).then_inc(T["v_ld"], 16)
            for t in range(B):
                sp.wait_ge(T["og"], t + 1)
                sp.dma_start(o_dram[t].rearrange("(g t) (h e) -> (t h) g e", t=TG, h=H), og[:, t, :, :]).then_inc(T["o_st"], 16)
                sp.wait_ge(T["o_st"], 16 * (t + 1))
                sp.dma_start(o2[:, t, :], o_dram[t]).then_inc(T["o_ld"], 16)
            for t in range(B):
                sp.wait_ge(T["fin"], t + 1)
                sp.dma_start(out[t * LQ:(t + 1) * LQ, :], fin[:, t, :]).then_inc(T["out"], 16)
            sp.wait_ge(T["out"], 16 * B)

        @block.tensor
        def _(pe):
            def x_transposed():
                pe.wait_ge(in_small, 32)
                for t in range(B):
                    pe.wait_ge(ln_out, t + 1)
                    for kt in range(KT):
                        last = pe.transpose(ps[:, 6 + t, kt * P:kt * P + P], xn0[:, t, kt * P:kt * P + P], id32[:, :])
                    last.then_inc(ln_t, 1)

            def project_q():
                pe.wait_ge(in_wq, 16)
                pe.wait_ge(ln_tc, B)
                for m in range(MT):
                    for kt in range(KT):
                        last = pe.matmul(ps[:, (0, 1, 6, 7)[m], 0:B * LQ], wq_sb[:, kt, m * P:m * P + P],
                                         xn0_t[:, kt, :, :].rearrange("p b q -> p (b q)"), start=kt == 0, stop=kt == KT - 1)
                    last.then_inc(q_mm, 1)

            def project(b, c, u):
                n, s = unit_no(b, c, u), c % 2
                if n >= 4:
                    pe.wait_ge(unit_lo, n - 3)
                for i, (wh, xh) in enumerate(((0, 0), (0, 1), (1, 0))):
                    if u == 0 and i == 0:
                        pe.wait_ge(c_hi_set, b * NCH + c + 1)
                    if u == 0 and i == 1:
                        pe.wait_ge(c_lo_set, b * NCH + c + 1)
                    if n == 0 or n == MT:
                        pe.wait_ge(w_lo_set if wh else w_hi_set, 1 + (n == MT))
                    if b and c == 0 and u == 0 and wh:
                        pe.wait_ge(wk_lo_back, 16)
                    for kt in range(KT):
                        if u >= MT:
                            tt = u - MT
                            lhs = (c_lo if xh else c_hi)[:, s, kt, tt * P:tt * P + P]
                            rhs = (wv_lo if wh else wv_hi)[:, kt, :]
                        else:
                            lhs = (wk_lo if wh else wk_hi)[:, kt, u * P:u * P + P]
                            rhs = (c_lo if xh else c_hi)[:, s, kt, :]
                        last = pe.matmul(ps[:, UB + n % 4, :], lhs, rhs, start=i == 0 and kt == 0, stop=i == 2 and kt == KT - 1)
                last.then_inc(unit_mm, 1)

            def scores(b, h, pair):
                g = b * H + h
                if pair == 0:
                    pe.wait_ge(k_stacked[h % NSLOT], 48 * (g // NSLOT + 1))
                    if h < NSLOT:
                        pe.wait_ge(ones_set, NSLOT * b + h + 1)
                    if h == 0:
                        pe.wait_ge(zeros_set, b + 1)
                for i in (2 * pair, 2 * pair + 1):
                    s = 4 * g + i
                    if s >= 2:
                        pe.wait_ge(s_max, s - 1)
                    pe.matmul(ps[:, s % 2, :], q_stack[:, h, :], k_slot(h)[:, i * CH:(i + 1) * CH],
                              start=True, stop=True).then_inc(s_mm, 1)

            def max_row(b, h):
                g = b * H + h
                pe.wait_ge(m_lo, g + 1)
                if g:
                    pe.wait_ge(m_row, g)
                pe.matmul(ps[:, 7, 0:P], m_cols[:, g % 2, :], id_r[:, :], start=True, stop=True).then_inc(m_mm, 1)

            def scores_t(b, h, i):
                g = b * H + h
                x_ = 2 * g + i
                if i == 0:
                    pe.wait_ge(m_row, g + 1)
                if x_ >= 2:
                    pe.wait_ge(p_exp, 2 * (x_ - 1))
                for k in range(HALF):
                    kt = i * HALF + k
                    last = pe.matmul(ps[:, 2 + 2 * (x_ % 2) + k // 4, (k % 4) * LQ:(k % 4) * LQ + LQ],
                                     k_slot(h)[:, kt * P:kt * P + P], q_stack[:, h, :], start=True, stop=True)
                last.then_inc(st_mm, 1)

            def weighted(b, h, i):
                g = b * H + h
                x_ = 2 * g + i
                if g % HPT == 0 and i == 0 and g:
                    pe.wait_ge(a_out, g // HPT)
                col = (h % HPT) * VC
                pe.wait_ge(p_low[i], g + 1)
                for k in range(HALF):
                    kt = i * HALF + k
                    pe.matmul(ps[:, 6, col:col + VC], p_hi[:, x_ % 3, k * LQ:k * LQ + LQ],
                              v_parts[:, kt, h, :], start=kt == 0, stop=False)
                    last = pe.matmul(ps[:, 6, col + HD:col + VC], p_lo[:, x_ % 3, k * LQ:k * LQ + LQ],
                                     v_parts[:, kt, h, HD:VC], start=False, stop=kt == NKT - 1)
                last.then_inc(pv_mm, 1)

            for b in range(B):
                for c in range(NCH):
                    for u in range(UNITS):
                        project(b, c, u)
                        if b == 0 and c == 0 and u == MT - 1:
                            x_transposed()
                        if b == 0 and c == 0 and u == MT + 1:
                            project_q()
                        if c == NCH - 1 and u >= MT + 1:
                            if u == MT + 1:
                                pe.wait_ge(q_stacked, 16 * 12 * (b + 1))
                            if u < UNITS - 1:
                                scores(b, 0, u - MT - 1)
                max_row(b, 0)
                scores(b, 1, 0)
                pe.wait_ge(unit_lo, (b + 1) * NCH * UNITS)
                scores_t(b, 0, 0)
                scores(b, 1, 1)
                scores(b, 2, 0)
                scores_t(b, 0, 1)
                max_row(b, 1)
                scores(b, 2, 1)
                pe.wait_ge(v_low, (b + 1) * NCH * TT)
                pe.wait_ge(const_set, 1)
                for h in range(1, H):
                    for i in range(2):
                        scores_t(b, h, i)
                        if h + 2 < H:
                            scores(b, h + 2, i)
                        if i == 0 and h + 1 < H:
                            max_row(b, h + 1)
                        weighted(b, h - 1, i)
                for i in range(2):
                    weighted(b, H - 1, i)

            def gemm(o, lhs, rhs):
                for kt in range(KT):
                    last = pe.matmul(o, lhs(kt), rhs(kt), start=kt == 0, stop=kt == KT - 1)
                return last

            def transposes(t, src, done):
                for kt in range(KT):
                    last = pe.transpose(ps[:, t, kt * P:kt * P + P], src[:, t, kt * P:kt * P + P], id32[:, :])
                last.then_inc(done, 1)

            pe.wait_ge(s_max, 4 * B * H)
            for t in range(B):
                pe.wait_ge(T["a"], t + 1)
                transposes(t, a_t, T["a_tr"])
            pe.wait_ge(T["in_w0"], 16)
            for t in range(B):
                pe.wait_ge(T["a_tc"], t + 1)
                gemm(ps[:, 2 + t, :], lambda kt: a_tt[:, t, kt, :], lambda kt: wo_sb[:, kt, :]).then_inc(T["y"], 1)
            for t in range(B):
                pe.wait_ge(T["xn"], t + 1)
                transposes(t, xn1, T["tr"])
            pe.wait_ge(T["tc"], B)
            for t in range(B):
                for i, w in enumerate((w_v_sb, w_k_sb, w_q_sb)):
                    pe.wait_ge(T[f"in_w{3 - i}"], 16)
                    gemm(ps[:, (4 + 3 * t + i) % 8, :], lambda kt: xn1_t[:, t, kt, :], lambda kt: w[:, kt, :]).then_inc(T["qkv"], 1)
            for t in range(B):
                pe.wait_ge(T["soft"], 2 * t + 2)
                for i in range(4):
                    n = 4 * t + i
                    for src, bank, freed in ((sq, 2, T["q_tc"]), (sk, 3, T["k_tc"])):
                        if n:
                            pe.wait_ge(freed, n)
                        for j in range(4):
                            h = 4 * i + j
                            last = pe.transpose(ps[0:HD, bank, j * P:j * P + P], src[:, t, h * HD:h * HD + HD], id32[:, :])
                        last.then_inc(T["qt_mm"], 1)
                pe.wait_ge(T["q_tc"], 4 * t + 4)
                pe.wait_ge(T["k_tc"], 4 * t + 4)
                if t == 0:
                    pe.wait_ge(T["sub"], 2)
                for i in range(NG // 4):
                    n = t * (NG // 4) + i
                    if n >= 2:
                        pe.wait_ge(T["g_m"], n - 1)
                    for j in range(4):
                        g = 4 * i + j
                        last = pe.matmul(ps[:, 5 + n % 2, j * P:j * P + P],
                                         k_t[:, t, g * TG:(g + 1) * TG, :].rearrange("p t h -> p (t h)"),
                                         q_t[:, t, g * TG:(g + 1) * TG, :].rearrange("p t h -> p (t h)"),
                                         start=True, stop=True)
                    last.then_inc(T["g_mm"], 1)
                pe.wait_ge(T["v_ld"], 16 * (t + 1))
                pe.wait_ge(T["g_m"], (t + 1) * (NG // 4))
                if t == 0:
                    pe.wait_ge(T["v_sb"], 2)
                for g in range(NG):
                    last = pe.matmul(ps[:, (4, 7)[t], g * HD:(g + 1) * HD], g_m[:, t, g, :], vs[:, t, g, :], start=True, stop=True)
                last.then_inc(T["o_mm"], 1)
            for t in range(B):
                pe.wait_ge(T["xn2"], t + 1)
                transposes(t, xn2, T["tr2"])
            pe.wait_ge(T["in_w4"], 16)
            for m in range(MT):
                if m == 0:
                    pe.wait_ge(T["mix_k"], KT)
                gemm(ps[:, 2 + m, 0:B * LQ], lambda kt: f_k_sb[:, kt, m * P:m * P + P],
                     lambda kt: xk[:, kt, :, :].rearrange("p b q -> p (b q)")).then_inc(T["k_mm"], 1)
            pe.wait_ge(T["in_w5"], 16)
            pe.wait_ge(T["mix_r"], KT)
            for t in range(B):
                gemm(ps[:, 6 + t, :], lambda kt: xr[:, kt, t, :], lambda kt: f_r_sb[:, kt, :]).then_inc(T["r_mm"], 1)
            pe.wait_ge(T["in_w6"], 16)
            pe.wait_ge(T["ka"], MT)
            for t in range(B):
                gemm(ps[:, t, :], lambda kt: ka[:, kt, t, :], lambda kt: f_v_sb[:, kt, :]).then_inc(T["f_mm"], 1)

        @block.scalar
        def _(act):
            def chunk_hi(n):
                act.wait_ge(in_chunk, 16 * (n + 1))
                if n % NCH >= 2:
                    act.wait_ge(unit_mm, (n - 1) * UNITS)
                elif n >= NCH:
                    act.wait_ge(st_mm, 2 * (n // NCH * H - NSLOT + 2 + n % NCH))
                act.activation(c_hi[:, n % 2, :, :], c_raw[:, :, :], ACT.Copy).then_inc(c_hi_set, 1)

            def x_std():
                act.wait_ge(eps_set, 1)
                for t in range(B):
                    act.wait_ge(ln_stat, t + 1)
                    act.activation(std[:, t:t + 1], mv[:, t, 1:2], ACT.Sqrt, bias=eps[:, :]).then_inc(ln_std, 1)

            def x_transposed():
                for t in range(B):
                    act.wait_ge(ln_t, t + 1)
                    act.activation(xn0_t[:, :, t, :], ps[:, 6 + t, :].rearrange("p (k q) -> p k q", k=KT), ACT.Copy).then_inc(ln_tc, 1)

            def project_q():
                for m in range(MT):
                    act.wait_ge(q_mm, m + 1)
                    act.activation(qa[:, :, m * P:m * P + P],
                                   ps[:, (0, 1, 6, 7)[m], 0:B * LQ].rearrange("p (b q) -> p b q", b=B),
                                   ACT.Identity, bias=colt[:, 0, m:m + 1]).then_inc(q_out, 1)
                act.wait_ge(q_out, MT)

            def q_high(b):
                if b:
                    act.wait_ge(pv_mm, 2 * H * b)
                act.activation(q_hi[:, :], qa[:, b, :], ACT.Copy).then_inc(q_hi_set, 1)

            def v_middle(n):
                v = v_units(n)
                act.wait_ge(unit_lo, n + 1)
                act.activation(v_parts[:, v % NKT, :, 2 * HD:3 * HD],
                               r1[:, v % 2, :].rearrange("p (h e) -> p h e", h=H), ACT.Copy).then_inc(v_mid, 1)

            def exps(g, i):
                x_ = 2 * g + i
                act.wait_ge(st_mm, x_ + 1)
                src = ps[:, 2 + 2 * (x_ % 2):4 + 2 * (x_ % 2), :].rearrange("p b c -> p (b c)")
                if g:
                    act.wait_ge(p_low[i], g)
                act.activation(p_full[:, x_ % 2, :], src, ACT.Exp, scale=SCALE).then_inc(p_exp, 1)
                if x_ >= 3:
                    act.wait_ge(pv_mm, x_ - 2)
                act.activation(p_hi[:, x_ % 3, :], src, ACT.Exp, scale=SCALE).then_inc(p_exp, 1)

            def max_row(b, h):
                g = b * H + h
                act.wait_ge(m_mm, g + 1)
                act.activation(q_stack[SR:P, h, :], ps[SR:P, 7, 0:LQ], ACT.Copy).then_inc(m_row, 1)

            act.wait_ge(in_wk, 16)
            act.activation(wk_hi[:, :, :], w_raw[:, 0, :, :], ACT.Copy).then_inc(w_hi_set, 1)
            chunk_hi(0)
            act.wait_ge(in_wv, 16)
            act.activation(wv_hi[:, :, :], w_raw[:, 1, :, :], ACT.Copy).then_inc(w_hi_set, 1)
            x_std()
            act.wait_ge(in_small, 32)
            for b in range(B):
                if b:
                    chunk_hi(b * NCH)
                    q_high(b)
                for c in range(NCH):
                    for u in range(UNITS):
                        n = unit_no(b, c, u)
                        if c == NCH - 1 and u == MT:
                            if b:
                                act.wait_ge(exp_loaded, b)
                            act.activation(warm[:, :], eps[:, :], ACT.Exp).then_inc(exp_loaded, 1)
                        act.wait_ge(unit_mm, n + 1)
                        if u >= MT:
                            if n == MT:
                                act.wait_ge(w_lo_set, 2)
                            act.activation(v_parts[:, c * TT + u - MT, :, HD:2 * HD],
                                           ps[:, UB + n % 4, :].rearrange("p (h e) -> p h e", h=H), ACT.Copy).then_inc(unit_hi, 1)
                            if u > MT:
                                v_middle(n - 1)
                            if u == UNITS - 1:
                                v_middle(n)
                        else:
                            act.activation(k_hi[:, u, c * CH:(c + 1) * CH], ps[:, UB + n % 4, :], ACT.Identity,
                                           bias=colt[:, 1, u:u + 1]).then_inc(unit_hi, 1)
                        if b == 0 and c == 0 and u == MT - 1:
                            x_transposed()
                        if b == 0 and c == 0 and u == MT + 1:
                            project_q()
                            q_high(0)
                        if u == 1 and c + 1 < NCH:
                            chunk_hi(b * NCH + c + 1)
                max_row(b, 0)
                exps(b * H, 0)
                exps(b * H, 1)
                max_row(b, 1)
                for h in range(1, H):
                    exps(b * H + h, 0)
                    if h + 1 < H:
                        max_row(b, h + 1)
                    exps(b * H + h, 1)

            for t in range(B):
                act.wait_ge(T["a_tr"], t + 1)
                act.activation(a_tt[:, t, :, :].rearrange("p k q -> p (k q)"), ps[:, t, :], ACT.Copy).then_inc(T["a_tc"], 1)
            for t in range(B):
                act.wait_ge(T["ln"], t + 1)
                act.activation(std[:, t:t + 1], mv[:, t, 1:2], ACT.Sqrt, bias=eps[:, :]).then_inc(T["std"], 1)
            for t in range(B):
                act.wait_ge(T["tr"], t + 1)
                act.activation(xn1_t[:, t, :, :].rearrange("p k q -> p (k q)"), ps[:, t, :], ACT.Copy).then_inc(T["tc"], 1)
            for t in range(B):
                act.wait_ge(T["qkv"], 3 * t + 1)
                act.activation(v_sb[:, t, :], ps[:, 4 + 3 * t, :], ACT.Copy).then_inc(T["v_sb"], 1)
                for i, s_ in enumerate((sk, sq)):
                    act.wait_ge(T["sub"], 2 * t + i + 1)
                    act.activation(s_[:, t, :], s_[:, t, :], ACT.Exp).then_inc(T["exp"], 1)
            for t in range(B):
                for i in range(4):
                    act.wait_ge(T["qt_mm"], 8 * t + 2 * i + 1)
                    act.activation(q_t[:, t, :, 4 * i:4 * i + 4].rearrange("p q h -> p h q"),
                                   ps[0:HD, 2, :].rearrange("p (h q) -> p h q", h=4), ACT.Copy).then_inc(T["q_tc"], 1)
                act.wait_ge(T["o_mm"], t + 1)
                act.activation(og[:, t, :, :].rearrange("p g e -> p (g e)"), ps[:, (4, 7)[t], :], ACT.Copy).then_inc(T["og"], 1)
            for t in range(B):
                act.wait_ge(T["x2"], 2 * t + 2)
                act.activation(std[:, t:t + 1], mv[:, t, 1:2], ACT.Sqrt, bias=eps[:, :]).then_inc(T["std2"], 1)
            act.wait_ge(T["zero"], 1)
            for t in range(B):
                act.wait_ge(T["tr2"], t + 1)
                act.activation(xp_t[:, :, t, 1:LQ + 1], ps[:, t, :].rearrange("p (k q) -> p k q", k=KT), ACT.Copy).then_inc(T["xp"], 1)
            act.wait_ge(T["xp"], B)
            act.wait_ge(T["om"], 1)
            for i in (1, 0):
                for kt in range(KT):
                    act.activation(prev[:, i, kt, :, :], xp_t[:, kt, :, 0:LQ], ACT.Copy, scale=om[:, i, kt:kt + 1]).then_inc(T["prev"], 1)
            for m in range(MT):
                act.wait_ge(T["k_mm"], m + 1)
                act.activation(relu[:, m, :, :].rearrange("p b q -> p (b q)"), ps[:, 2 + m, 0:B * LQ], ACT.Relu).then_inc(T["relu"], 1)
            for t in range(B):
                act.wait_ge(T["r_mm"], t + 1)
                act.activation(gate[:, t, :], ps[:, 6 + t, :], ACT.Sigmoid).then_inc(T["gate"], 1)

        @block.vector
        def _(dve):
            chain = [0]

            def link(ins):
                chain[0] += 1
                ins.then_inc(dve_chain, 1)
                dve.wait_ge(dve_chain, chain[0])

            dve.memset(eps[:, :], EPS).then_inc(eps_set, 1)
            def chunk_lo(n):
                dve.wait_ge(c_hi_set, n + 1)
                if n // NCH and n % NCH < 2:
                    if n % NCH == 0:
                        dve.wait_ge(p_low[0], H * (n // NCH))
                        dve.wait_ge(p_low[1], H * (n // NCH))
                    else:
                        dve.wait_ge(pv_mm, 2 * H * (n // NCH))
                dve.tensor_tensor(c_lo[:, n % 2, :, :], c_raw[:, :, :], c_hi[:, n % 2, :, :].bitcast(F32),
                                  ALU.subtract).then_inc(c_lo_set, 1)

            def x_norm():
                dve.wait_ge(in_x, 16)
                for t in range(B):
                    link(dve.bn_stats(stat[:, t, :], x_in[:, t, :]))
                    dve.bn_aggr(mv[:, t, :], stat[:, t, :]).then_inc(ln_stat, 1)
                dve.wait_ge(ln_stat, B)
                for t in range(B):
                    dve.wait_ge(ln_std, t + 1)
                    link(dve.reciprocal(rstd[:, t:t + 1], std[:, t:t + 1]))
                    dve.tensor_scalar(xn0[:, t, :], x_in[:, t, :], mv[:, t, 0:1], rstd[:, t:t + 1],
                                      ALU.subtract, ALU.mult).then_inc(ln_out, 1)
                dve.wait_ge(in_small, 32)
                link(dve.tensor_copy(id_r[:, :], id32[:, :]))

            def q_low(b):
                dve.wait_ge(q_hi_set, b + 1)
                dve.tensor_tensor(q_lo[:, :], qa[:, b, :], q_hi[:, :].bitcast(F32), ALU.subtract).then_inc(q_lo_set, 1)

            def maxima(b, h, pair):
                g = b * H + h
                if g and pair == 0:
                    dve.wait_ge(m_lo, g)
                for i in (2 * pair, 2 * pair + 1):
                    dve.wait_ge(s_mm, 4 * g + i + 1)
                    dve.tensor_reduce(pm[:, i:i + 1], ps[:, (4 * g + i) % 2, :], AX_X, ALU.max).then_inc(s_max, 1)

            def maximum(b, h):
                g = b * H + h
                dve.wait_ge(s_max, 4 * g + 4)
                dve.tensor_reduce(m_q[:, :], pm[:, :], AX_X, ALU.max).then_inc(m_red, 1)
                dve.wait_ge(m_red, g + 1)
                if g >= 2:
                    dve.wait_ge(m_mm, g - 1)
                dve.tensor_scalar(m_cols[:, g % 2, SR:SR + 1], m_q[:, :], -1.0, LIFT, ALU.mult, ALU.add).then_inc(m_hi, 1)
                dve.tensor_scalar(pm[:, 0:1], m_q[:, :], -1.0, LIFT, ALU.mult, ALU.add).then_inc(m_hi, 1)
                dve.wait_ge(m_hi, 2 * g + 2)
                dve.tensor_tensor(m_cols[:, g % 2, SR + 1:SR + 2], pm[:, 0:1],
                                  m_cols[:, g % 2, SR:SR + 1].bitcast(F32), ALU.subtract).then_inc(m_lo, 1)

            def lows(b, h):
                x_ = 2 * (b * H + h)
                dve.wait_ge(p_exp, 2 * (x_ + 1))
                if x_ >= 3:
                    dve.wait_ge(pv_mm, x_ - 2)
                dve.tensor_tensor(p_lo[:, x_ % 3, :], p_full[:, 0, :], p_hi[:, x_ % 3, :], ALU.subtract).then_inc(p_low[0], 1)

            def gather(b, m):
                k = b * MT + m
                dve.wait_ge(pv_mm, 2 * HPT * (k + 1))
                acc = ps[:, 6, 0:HPT * VC].rearrange("p (j c) -> p j c", j=HPT)
                dst = qa[:, b, m * P:m * P + P].rearrange("p (j e) -> p j e", j=HPT)
                link(dve.tensor_reduce(dst, acc[:, :, 0:3 * HD].rearrange("p j (c e) -> p j e c", c=3), AX_X, ALU.add))
                link(dve.reciprocal(rec[:, :], acc[:, :, VC - 1]))
                for j in range(HPT):
                    last = dve.tensor_scalar(dst[:, j, :], dst[:, j, :], rec[:, j:j + 1], None, ALU.mult)
                last.then_inc(a_out, 1)
                dve.wait_ge(a_out, k + 1)

            dve.wait_ge(w_hi_set, 1)
            dve.tensor_tensor(wk_lo[:, :, :], w_raw[:, 0, :, :], wk_hi[:, :, :].bitcast(F32), ALU.subtract).then_inc(w_lo_set, 1)
            chunk_lo(0)
            dve.wait_ge(w_hi_set, 2)
            dve.tensor_tensor(wv_lo[:, :, :], w_raw[:, 1, :, :], wv_hi[:, :, :].bitcast(F32), ALU.subtract).then_inc(w_lo_set, 1)
            x_norm()
            for b in range(B):
                if b:
                    chunk_lo(b * NCH)
                    gather(b - 1, MT - 1)
                    q_low(b)
                for c in range(NCH):
                    for u in range(UNITS):
                        n = unit_no(b, c, u)
                        dve.wait_ge(unit_hi, n + 1)
                        if u >= MT:
                            v = v_units(n)
                            if v >= 2:
                                dve.wait_ge(v_low, v - 1)
                            dve.tensor_tensor(r1[:, v % 2, :].rearrange("p (h e) -> p h e", h=H),
                                              ps[:, UB + n % 4, :].rearrange("p (h e) -> p h e", h=H),
                                              v_parts[:, v % NKT, :, HD:2 * HD], ALU.subtract).then_inc(unit_lo, 1)
                        else:
                            dve.scalar_tensor_tensor(k_lo[:, u, c * CH:(c + 1) * CH], ps[:, UB + n % 4, :], colt[:, 1, u:u + 1],
                                                     k_hi[:, u, c * CH:(c + 1) * CH].bitcast(F32),
                                                     ALU.add, ALU.subtract).then_inc(unit_lo, 1)
                        if b == 0 and c == 0 and u == MT + 1:
                            q_low(0)
                        if u == 1 and c + 1 < NCH:
                            chunk_lo(b * NCH + c + 1)
                        if c == NCH - 1 and MT + 1 <= u < UNITS - 1:
                            if b == 0:
                                dve.wait_ge(const_set, 2)
                            maxima(b, 0, u - MT - 1)
                            if u == UNITS - 2:
                                maximum(b, 0)
                maxima(b, 1, 0)
                maxima(b, 1, 1)
                maximum(b, 1)
                for h in range(H):
                    if h >= 5 and (h - 5) % HPT == 0:
                        gather(b, (h - 5) // HPT)
                    if h + 2 < H:
                        maxima(b, h + 2, 0)
                    if h + 2 < H:
                        maxima(b, h + 2, 1)
                        maximum(b, h + 2)
                    lows(b, h)
            gather(B - 1, MT - 1)

            dve.wait_ge(T["in_rows"], 16)
            for t in range(B):
                dve.tensor_tensor(a_t[:, t, :], qa[:, t, :], bias_rows[:, 0, :], ALU.add).then_inc(T["a"], 1)

            def layernorm(t, src, dst, stat_done, std_done, out_done):
                link(dve.bn_stats(stat[:, t, :], src[:, t, :]))
                dve.bn_aggr(mv[:, t, :], stat[:, t, :]).then_inc(stat_done, 1)

            def normalise(t, src, dst, std_done, out_done):
                dve.wait_ge(std_done, t + 1)
                link(dve.reciprocal(rstd[:, t:t + 1], std[:, t:t + 1]))
                dve.tensor_scalar(dst[:, t, :], src[:, t, :], mv[:, t, 0:1], rstd[:, t:t + 1],
                                  ALU.subtract, ALU.mult).then_inc(out_done, 1)

            dve.wait_ge(T["xo"], 2)
            for t in range(B):
                dve.wait_ge(T["y"], t + 1)
                link(dve.tensor_tensor(x1[:, t, :], ps[:, 2 + t, :], xo[:, t, :], ALU.add))
                layernorm(t, x1, xn1, T["ln"], None, None)
            dve.wait_ge(T["ln"], B)
            for t in range(B):
                normalise(t, x1, xn1, T["std"], T["xn"])

            def groups(t, i):
                bank = (4 + 3 * t + 1 + i) % 8
                s_ = (sk, sq)[i]
                if i == 0:
                    v = lambda a: a.rearrange("p (h e) -> p e h", h=H)
                    lo, hi = 0, HD
                else:
                    v = lambda a: a.rearrange("p (h e) -> p h e", h=H)
                    lo, hi = HD, HD + H
                return v(ps[:, bank, :]), v(s_[:, t, :]), slice(lo, hi)

            def spread(a, n):
                return a.unsqueeze(2).to_broadcast([P, a.shape[1], n])

            dve.wait_ge(m_mm, B * H)
            for t in range(B):
                for i in range(2):
                    dve.wait_ge(T["qkv"], 3 * t + i + 2)
                    src, dst, c = groups(t, i)
                    link(dve.tensor_reduce(mx[:, t, c], src, AX_X, ALU.max))
                    dve.tensor_tensor(dst, src, spread(mx[:, t, c], src.shape[2]), ALU.subtract).then_inc(T["sub"], 1)
            for t in range(B):
                for i in range(2):
                    dve.wait_ge(T["exp"], 2 * t + i + 1)
                    src, dst, c = groups(t, i)
                    link(dve.tensor_reduce(sm[:, t, c], dst, AX_X, ALU.add))
                    link(dve.reciprocal(rs[:, t, c], sm[:, t, c]))
                    dve.tensor_tensor(dst, dst, spread(rs[:, t, c], dst.shape[2]), ALU.mult).then_inc(T["soft"], 1)
            dve.wait_ge(T["in_mask"], 16)
            for t in range(B):
                for i in range(4):
                    dve.wait_ge(T["qt_mm"], 8 * t + 2 * i + 2)
                    dve.tensor_copy(k_t[:, t, :, 4 * i:4 * i + 4].rearrange("p q h -> p h q"),
                                    ps[0:HD, 3, :].rearrange("p (h q) -> p h q", h=4)).then_inc(T["k_tc"], 1)
                for i in range(NG // 4):
                    n = t * (NG // 4) + i
                    dve.wait_ge(T["g_mm"], n + 1)
                    dve.tensor_tensor(g_m[:, t, 4 * i:4 * i + 4, :].rearrange("p g c -> p (g c)"), ps[:, 5 + n % 2, :],
                                      maskt[:, :, :].rearrange("p g c -> p (g c)"), ALU.mult).then_inc(T["g_m"], 1)
            for t in range(B):
                dve.wait_ge(T["o_ld"], 16 * (t + 1))
                dve.tensor_tensor(x2[:, t, :], x1[:, t, :], o2[:, t, :], ALU.add).then_inc(T["x2"], 1)
                dve.wait_ge(T["x2"], 2 * t + 1)
                layernorm(t, x2, xn2, T["x2"], None, None)
            dve.wait_ge(T["x2"], 2 * B)
            for t in range(B):
                normalise(t, x2, xn2, T["std2"], T["xn2"])
            dve.wait_ge(T["xp"], B)
            dve.wait_ge(T["o_mm"], B)
            for n, (i, dst, done) in enumerate(((1, xk, T["mix_k"]), (0, xr, T["mix_r"]))):
                for kt in range(KT):
                    dve.wait_ge(T["prev"], n * KT + kt + 1)
                    dve.scalar_tensor_tensor(dst[:, kt, :, :], xp_t[:, kt, :, 1:LQ + 1], colt[:, 2 + i, kt:kt + 1],
                                             prev[:, i, kt, :, :], ALU.mult, ALU.add).then_inc(done, 1)
            for m in range(MT):
                dve.wait_ge(T["relu"], m + 1)
                dve.tensor_tensor(ka[:, m, :, :], relu[:, m, :, :], relu[:, m, :, :], ALU.mult).then_inc(T["ka"], 1)
            for t in range(B):
                dve.wait_ge(T["gate"], t + 1)
                dve.wait_ge(T["f_mm"], t + 1)
                link(dve.tensor_tensor(fin[:, t, :], ps[:, t, :], gate[:, t, :], ALU.mult))
                dve.tensor_tensor(fin[:, t, :], fin[:, t, :], x2[:, t, :], ALU.add).then_inc(T["fin"], 1)

        @block.gpsimd
        def _(pool):
            def v_lowest(n):
                v = v_units(n)
                pool.wait_ge(v_mid, v + 1)
                pool.tensor_tensor(v_parts[:, v % NKT, :, 0:HD], r1[:, v % 2, :].rearrange("p (h e) -> p h e", h=H),
                                   v_parts[:, v % NKT, :, 2 * HD:3 * HD], ALU.subtract).then_inc(v_low, 1)

            def ones(b, i):
                pool.memset(k_slot(i)[SR:P, :].bitcast(F32), 1.0).then_inc(ones_set, 1)
                pool.wait_ge(ones_set, NSLOT * b + i + 1)

            for b in range(B):
                for c in range(NCH):
                    if c == 1:
                        if b:
                            pool.wait_ge(st_mm, 2 * H * b)
                        else:
                            pool.wait_ge(T["om"], 1)
                        pool.wait_ge(v_low, v_units(unit_no(b, c, 0)))
                        pool.memset(q_stack[SR:P, :, :].bitcast(F32), 0.0).then_inc(zeros_set, 1)
                        pool.wait_ge(zeros_set, b + 1)
                    for u in range(MT, UNITS):
                        v_lowest(unit_no(b, c, u))
                        if c == NCH - 1 and u < MT + 2:
                            pool.wait_ge(c_lo_set, (b + 1) * NCH)
                            pool.wait_ge(unit_mm, unit_no(b, c, 0))
                            pool.wait_ge(v_low, v_units(unit_no(b, c, u)) + 1)
                            ones(b, u - MT)
                    if b == 0 and c == 0:
                        pool.wait_ge(q_mm, MT)
                        pool.wait_ge(v_low, TT)
                        pool.memset(v_parts[:, :, :, VC - 1], 1.0).then_inc(const_set, 1)
                        pool.memset(m_cols[:, :, :].bitcast(F32), 0.0).then_inc(const_set, 1)
                        pool.wait_ge(in_small, 32)
                        pool.tensor_scalar(om[:, :, :], colt[:, 2:4, :], -1.0, 1.0, ALU.mult, ALU.add).then_inc(T["om"], 1)
                pool.wait_ge(unit_mm, (b + 1) * NCH * UNITS)
                pool.wait_ge(v_low, (b + 1) * NCH * TT)
                pool.wait_ge(wk_lo_kept, 16)
                ones(b, 2)
                ones(b, 3)
                for h in range(H):
                    x_ = 2 * (b * H + h) + 1
                    pool.wait_ge(p_exp, 2 * (x_ + 1))
                    if x_ >= 3:
                        pool.wait_ge(pv_mm, x_ - 2)
                    pool.tensor_tensor(p_lo[:, x_ % 3, :], p_full[:, 1, :], p_hi[:, x_ % 3, :], ALU.subtract).then_inc(p_low[1], 1)
            pool.wait_ge(T["in_x"], 16)
            pool.wait_ge(T["in_rows"], 16)
            for t in range(B):
                pool.tensor_tensor(xo[:, t, :], x_res[:, t, :], bias_rows[:, 1, :], ALU.add).then_inc(T["xo"], 1)
            pool.wait_ge(pv_mm, 2 * B * H)
            pool.memset(xp_t[:, :, :, 0:1], 0.0).then_inc(T["zero"], 1)


def kernel(**inputs):
    import numpy as np
    import concourse.bacc as bacc
    from concourse.bass_utils import run_bass_kernel_spmd

    a = {k: np.asarray(v) for k, v in inputs.items()}

    def tiles(w):
        return np.ascontiguousarray(w.reshape(KT, P, D).transpose(1, 0, 2))

    def col(v):
        return v.reshape(KT, P).T

    ctx_in = a["ctx_1024"].reshape(B * NCH, CH, KT, P).transpose(0, 3, 2, 1)
    block = np.kron(np.eye(TG, dtype=np.float32), np.ones((H, H), np.float32))
    data = {
        "x": a["x"].reshape(B * LQ, D),
        "ctx_t": ctx_in,
        "wq": tiles(a["L0_xattn_Wq"]), "wk": tiles(a["L0_xattn_Wk"]), "wv": tiles(a["L0_xattn_Wv"]),
        "wo": tiles(a["L0_xattn_Wo"]),
        "w_q": tiles(a["L0_attn_W_Q"].T), "w_k": tiles(a["L0_attn_W_K"].T), "w_v": tiles(a["L0_attn_W_V"].T),
        "f_r": tiles(a["L0_ffn_W_r"].T), "f_k": tiles(a["L0_ffn_W_k"].T), "f_v": tiles(a["L0_ffn_W_v"].T),
        "cols": np.stack([col(a["L0_xattn_bq"]), col(a["L0_xattn_bk"]), col(a["L0_ffn_mu_r"]), col(a["L0_ffn_mu_k"])], 1),
        "rows": np.broadcast_to(np.stack([a["L0_xattn_bv"], a["L0_xattn_bo"]])[None], (P, 2, D)),
        "ident": np.eye(P, dtype=np.float32),
        "mask": np.broadcast_to(block[:, None, :], (P, 4, P)),
    }
    nc = bacc.Bacc("TRN2", target_bir_lowering=False, num_devices=1)
    arrays, args = {}, []
    for name, v in data.items():
        v = np.ascontiguousarray(v)
        arrays[f"in_{name}"] = v
        args.append(nc.dram_tensor(f"in_{name}", v.shape, F32, kind="ExternalInput").ap())
    out = nc.dram_tensor("out", [B * LQ, D], F32, kind="ExternalOutput").ap()
    perceiver(nc, *args, out)
    r = run_bass_kernel_spmd(nc, [arrays], core_ids=[0])
    return r.results[0]["out"].reshape(B, LQ, D)
```

```python
from contextlib import ExitStack

import concourse.bass as bass
from concourse import mybir

F32 = mybir.dt.float32
F32R = mybir.dt.float32r
BF16 = mybir.dt.bfloat16
F16 = mybir.dt.float16
ALU = mybir.AluOpType
ACT = mybir.ActivationFunctionType
AX_X = mybir.AxisListType.X

P = 128
B = 2
LQ = 128
D = 512
KT = D // P
LK = 2048
H = 16
HD = D // H
MT = D // P
HPT = P // HD
CH = 512
NCH = LK // CH
TT = CH // P
NKT = LK // P
UNITS = MT + TT
UB = 2
NSLOT = 4
VC = 3 * HD + 1
SR = 3 * HD
HALF = NKT // 2
FH = HALF * LQ
DF = FH // 2
TG = P // H
NG = LQ // TG
EPS = 1e-5
SCALE = 1.0 / HD ** 0.5
LIFT = 14 * 0.6931471805599453 / SCALE


def perceiver(nc, x, ctx_t, wq, wk, wv, wo, w_q, w_k, w_v, f_r, f_k, f_v, cols, rows, ident, mask, out):
    v_dram = nc.dram_tensor("v_rows", [B, LQ, D], F32, kind="Internal").ap()
    wk_lo_dram = nc.dram_tensor("wk_lo_kept", [P, KT * D], F32, kind="Internal").ap()
    o_dram = nc.dram_tensor("mixed_rows", [B, LQ, D], F32, kind="Internal").ap()

    with ExitStack() as ctx:
        def sem(name):
            return ctx.enter_context(nc.semaphore(name))

        base = (nc.sbuf_base + 31) // 32 * 32
        at = [base]

        def place(name, shape, dt, size=None):
            n = 1
            for s in shape[1:]:
                n *= s
            n *= 2 if dt in (BF16, F16) else 4
            t = nc.alloc_sbuf_tensor_at(name, shape, dt, offset=at[0])
            at[0] += (n + 31) // 32 * 32
            return t

        k_hi = place("k_hi", [P, MT, LK], F32R)
        k_lo = place("k_lo", [P, MT, LK], F32R)
        v_at = at[0]
        v_parts = place("v_parts", [P, NKT, H, VC], BF16)
        w_at = at[0]
        wk_hi = place("wk_hi", [P, KT, D], F32R)
        wk_lo_at = at[0]
        wk_lo = place("wk_lo", [P, KT, D], F32R)
        wv_hi = place("wv_hi", [P, KT, D], F32R)
        wv_lo = place("wv_lo", [P, KT, D], F32R)
        both_at = at[0]
        c_raw = place("c_raw", [P, KT, CH], F32)
        c_hi = place("c_hi", [P, 2, KT, CH], F32R)
        c_lo = place("c_lo", [P, 2, KT, CH], F32R)
        q_hi = place("q_hi", [P, D], F32R)
        q_lo = place("q_lo", [P, D], F32R)
        both_end = at[0]
        stacks = []
        for i, over in enumerate((0, 1, 3)):
            at[0] = both_at + over * KT * CH * 4
            stacks.append(place(f"k_stack{i}", [P, LK], F32R))
        at[0] = both_at + 2 * KT * CH * 4
        p_full = place("p_full", [P, 2, FH], F32)
        at[0] = both_at + 4 * KT * CH * 4
        p_hi = place("p_hi", [P, 3, FH], F16)
        p_lo = place("p_lo", [P, 3, FH], F16)
        assert at[0] <= both_end
        at[0] = wk_lo_at
        stacks.append(place("k_stack3", [P, LK], F32R))
        at[0] = both_end
        q_stack = place("q_stack", [P, H, LQ], F32R)
        qa = place("qa", [P, B, D], F32)
        r1 = place("r1", [P, 2, D], F32)
        id32 = place("id32", [P, P], F32)
        id_r = place("id_r", [P, P], F32R)
        m_cols = place("m_cols", [P, 2, P], F32R)
        colt = place("colt", [P, 4, KT], F32)
        om = place("om", [P, 2, KT], F32)
        stat = place("stat", [P, 2, 6], F32)
        mv = place("mv", [P, 2, 2], F32)
        std = place("std", [P, 2], F32)
        rstd = place("rstd", [P, 2], F32)
        eps = place("eps", [P, 1], F32)
        pm = place("pm", [P, 4], F32)
        m_q = place("m_q", [P, 1], F32)
        rec = place("rec", [P, 4], F32)
        warm = place("warm", [P, 1], F32)
        assert at[0] <= nc.sbuf_top, (at[0], nc.sbuf_top)

        at[0] = v_at
        w_raw = place("w_raw", [P, 2, KT, D], F32)
        wq_sb = place("wq_sb", [P, KT, D], F32)
        x_in = place("x_in", [P, B, D], F32)
        xn0 = place("xn0", [P, B, D], F32)
        xn0_t = place("xn0_t", [P, KT, B, LQ], F32)
        assert at[0] <= w_at
        at[0] = base
        names = ["wo_sb", "w_v_sb", "w_k_sb", "w_q_sb", "f_k_sb", "f_r_sb", "f_v_sb"]
        wo_sb, w_v_sb, w_k_sb, w_q_sb, f_k_sb, f_r_sb, f_v_sb = [place(n, [P, KT, D], F32) for n in names]
        assert at[0] <= v_at
        low_halves, high_halves = {}, {}
        for i, over in ((1, 3), (2, 0), (3, 1)):
            name = ("w_v", "w_k", "w_q")[i - 1]
            at[0] = base + i * KT * D * 4
            low_halves[name] = place(name + "_lo", [P, KT, D], F32R)
            at[0] = both_at + over * KT * CH * 4
            high_halves[name] = place(name + "_hi", [P, KT, D], F32R)
        at[0] = w_at
        x_res = place("x_res", [P, B, D], F32)
        bias_rows = place("bias_rows", [P, 2, D], F32)
        at[0] = w_at
        high_halves["f_r"] = place("f_r_hi", [P, KT, D], F32R)
        at[0] = base
        high_halves["f_v"] = place("f_v_hi", [P, KT, D], F32R)
        xr_hi = place("xr_hi", [P, B, KT, LQ], F32R)
        xr_lo = place("xr_lo", [P, B, KT, LQ], F32R)
        ka_hi = place("ka_hi", [P, B, MT, LQ], F32R)
        ka_lo = place("ka_lo", [P, B, MT, LQ], F32R)
        for i, name in ((5, "f_r"), (6, "f_v")):
            at[0] = base + i * KT * D * 4
            low_halves[name] = place(name + "_lo", [P, KT, D], F32R)
        at[0] = wk_lo_at
        maskt = place("maskt", [P, 4, P], F32)
        vs = place("vs", [P, B, NG, HD], F32)
        at[0] = wk_lo_at + 8192
        xo = place("xo", [P, B, D], F32)
        a_t = place("a_t", [P, B, D], F32)
        x1 = place("x1", [P, B, D], F32)
        xn1 = place("xn1", [P, B, D], F32)
        assert at[0] <= both_at
        at[0] = both_at + 2 * KT * CH * 4
        xn1_hi = place("xn1_hi", [P, B, KT, LQ], F32R)
        xn1_lo = place("xn1_lo", [P, B, KT, LQ], F32R)
        at[0] = both_at + 4 * KT * CH * 4
        og = place("og", [P, B, NG, HD], F32)
        o2 = place("o2", [P, B, D], F32)
        x2 = place("x2", [P, B, D], F32)
        assert at[0] <= both_end
        at[0] = both_at
        prev = place("prev", [P, 2, KT, B, LQ], F32)
        xn2 = place("xn2", [P, B, D], F32)
        at[0] = both_at + 3 * KT * CH * 4
        xp_t = place("xp_t", [P, KT, B, LQ + 1], F32)
        at[0] = v_at
        g_m = place("g_m", [P, B, NG, P], F32)
        q_t = place("q_t", [P, B, LQ, H], F32)
        k_t = place("k_t", [P, B, LQ, H], F32)
        assert at[0] <= w_at
        at[0] = v_at + B * NG * P * 4
        xr = place("xr", [P, B, KT, LQ], F32)
        xk = place("xk", [P, KT, B, LQ], F32)
        relu = place("relu", [P, B, MT, LQ], F32)
        ka = place("ka", [P, B, MT, LQ], F32)
        assert at[0] <= w_at
        at[0] = both_end
        gate = place("gate", [P, B, D], F32)
        fin = place("fin", [P, B, D], F32)
        at[0] = base + 7 * 8192
        a_tt = place("a_tt", [P, B, KT, LQ], F32)
        v_sb = place("v_sb", [P, B, D], F32)
        assert at[0] <= v_at
        at[0] = both_end + 8192
        sq = place("sq", [P, B, D], F32)
        sk = place("sk", [P, B, D], F32)
        at[0] = both_end + 8192 + 8192 + 512
        mx = place("mx", [P, B, 48], F32)
        sm = place("sm", [P, B, 48], F32)
        rs = place("rs", [P, B, 48], F32)

        ps = ctx.enter_context(nc.psum_tensor("ps", [P, 8, 512], F32))

        in_x, in_wq, in_wv = sem("in_x"), sem("in_wq"), sem("in_wv")
        in_first = [sem(f"in_first{kt}") for kt in range(KT)]
        first_hi, first_lo = sem("first_hi"), sem("first_lo")
        in_small = sem("in_small")
        in_chunk = sem("in_chunk")
        q_stacked = sem("q_stacked")
        k_stacked = [sem(f"k_stacked{i}") for i in range(NSLOT)]
        wk_lo_kept = sem("wk_lo_kept")
        wk_lo_back = sem("wk_lo_back")
        eps_set = sem("eps_set")
        const_set = sem("const_set")
        ones_set = sem("ones_set")
        zeros_set = sem("zeros_set")
        exp_loaded = sem("exp_loaded")
        w_hi_set, w_lo_set = sem("w_hi_set"), sem("w_lo_set")
        ln_stat, ln_std, ln_out, ln_t, ln_tc = sem("ln_stat"), sem("ln_std"), sem("ln_out"), sem("ln_t"), sem("ln_tc")
        q_mm, q_out = sem("q_mm"), sem("q_out")
        q_hi_set, q_lo_set = sem("q_hi_set"), sem("q_lo_set")
        c_hi_set, c_lo_set = sem("c_hi_set"), sem("c_lo_set")
        unit_mm = sem("unit_mm")
        unit_hi = sem("unit_hi")
        unit_lo = sem("unit_lo")
        v_mid, v_low = sem("v_mid"), sem("v_low")
        s_mm, s_max = sem("s_mm"), sem("s_max")
        m_red, m_hi, m_lo, m_mm, m_row = sem("m_red"), sem("m_hi"), sem("m_lo"), sem("m_mm"), sem("m_row")
        st_mm, p_exp, pv_mm = sem("st_mm"), sem("p_exp"), sem("pv_mm")
        low_dve, low_pool = sem("low_dve"), sem("low_pool")
        acc_read, a_out, dve_chain = sem("acc_read"), sem("a_out"), sem("dve_chain")

        def k_slot(h):
            return stacks[h % NSLOT][:, :]

        def unit_no(b, c, u):
            return (b * NCH + c) * UNITS + u

        def v_units(n):
            return n // UNITS * TT + max(n % UNITS - MT, 0)

        T = {n: sem("t_" + n) for n in (
            "in_wo in_w_k in_w_q in_w_v in_f_k in_f_r in_f_v in_x in_rows in_mask a a_tr a_tc y std ln xn tr tc x_lo w_k_hi w_k_lo w_q_hi w_q_lo w_v_hi w_v_lo f_r_hi f_r_lo f_v_hi f_v_lo xr_hi xr_lo ka_hi ka_lo v_mm kq_mm sub "
            "exp v_sb v_st v_ld soft kt_mm qt_mm q_tc k_tc g_mm g_m o_mm og o_st o_ld x2 ln2 std2 xn2 tr2 zero rows_zero xp prev mix_k mix_r "
            "k_mm r_mm relu ka gate f_mm fin out om").split()}

        block = ctx.enter_context(nc.Block())

        @block.sync
        def _(sp):
            def load_chunk(n):
                if n:
                    sp.wait_ge(c_hi_set, n)
                    sp.wait_ge(c_lo_set, n)
                if n == NCH:
                    sp.wait_ge(st_mm, 2 * (H - NSLOT + 1))
                sp.dma_start(c_raw[:, :, :], ctx_t[n]).then_inc(in_chunk, 16)

            for kt in range(KT):
                sp.dma_start(w_raw[:, 0, kt, :], wk[:, kt, :]).then_inc(in_first[kt], 16)
                sp.dma_start(c_raw[:, kt, :], ctx_t[0][:, kt, :]).then_inc(in_first[kt], 16)
            sp.dma_start(w_raw[:, 1, :, :], wv).then_inc(in_wv, 16)
            sp.dma_start(x_in[:, :, :], x.rearrange("(b p) d -> p b d", p=P)).then_inc(in_x, 16)
            sp.dma_start(colt[:, :, :], cols).then_inc(in_small, 16)
            sp.dma_start(id32[:, :], ident).then_inc(in_small, 16)
            sp.dma_start(wq_sb[:, :, :], wq).then_inc(in_wq, 16)

            for b in range(B):
                load_chunk(b * NCH + (b == 0))
                if b == 0:
                    sp.wait_ge(w_lo_set, 1)
                    sp.dma_start(wk_lo_dram, wk_lo[:, :, :].rearrange("p k n -> p (k n)").bitcast(F32)).then_inc(wk_lo_kept, 16)
                else:
                    sp.wait_ge(st_mm, 2 * H * b)
                    sp.wait_ge(wk_lo_kept, 16)
                    sp.dma_start(wk_lo[:, :, :].rearrange("p k n -> p (k n)").bitcast(F32), wk_lo_dram).then_inc(wk_lo_back, 16)
                    load_chunk(b * NCH + 1)
                load_chunk(b * NCH + 2)
                sp.wait_ge(q_hi_set, b + 1)
                sp.wait_ge(q_lo_set, b + 1)
                for j in range(HPT):
                    for r, part in enumerate((q_hi, q_hi, q_lo)):
                        dst = q_stack[HD * r:HD * r + HD, :, :].rearrange("p (m j) q -> p m j q", j=HPT)[:, :, j, :]
                        src = part[HD * j:HD * j + HD, :].rearrange("p (m q) -> p m q", m=MT)
                        sp.dma_start(dst.bitcast(F32), src.bitcast(F32)).then_inc(q_stacked, 16)
                load_chunk(b * NCH + 3)
                n = unit_no(b, NCH - 1, 0)
                sp.wait_ge(unit_hi, n + 1)
                sp.wait_ge(unit_lo, n + 1)
                sp.wait_ge(c_lo_set, (b + 1) * NCH)
                sp.wait_ge(unit_mm, n)
                for h in range(H):
                    g, m, j = b * H + h, h // HPT, h % HPT
                    if h == NSLOT - 1:
                        sp.wait_ge(wk_lo_kept, 16)
                        sp.wait_ge(unit_mm, n + MT)
                    if h == HPT:
                        sp.wait_ge(unit_hi, n + MT)
                        sp.wait_ge(unit_lo, n + MT)
                    if h >= NSLOT:
                        sp.wait_ge(st_mm, 2 * (g - NSLOT + 1))
                    if b == B - 1 and h == NSLOT:
                        sp.dma_start(x_res[:, :, :], x.rearrange("(b p) d -> p b d", p=P)).then_inc(T["in_x"], 16)
                        sp.dma_start(bias_rows[:, :, :], rows).then_inc(T["in_rows"], 16)
                    for r, part in enumerate((k_hi, k_lo, k_hi)):
                        sp.dma_start(k_slot(h)[HD * r:HD * r + HD, :].bitcast(F32),
                                     part[HD * j:HD * j + HD, m, :].bitcast(F32)).then_inc(k_stacked[h % NSLOT], 16)
                if b == B - 1:
                    for i in range(NSLOT):
                        sp.wait_ge(k_stacked[i], 48 * B * H // NSLOT)
                    for name, t, w in (("wo", wo_sb, wo), ("w_k", w_k_sb, w_k), ("w_q", w_q_sb, w_q), ("w_v", w_v_sb, w_v),
                                       ("f_k", f_k_sb, f_k), ("f_r", f_r_sb, f_r), ("f_v", f_v_sb, f_v)):
                        sp.dma_start(t[:, :, :], w).then_inc(T["in_" + name], 16)
                    sp.wait_ge(st_mm, 2 * B * H)
                    sp.dma_start(maskt[:, :, :], mask).then_inc(T["in_mask"], 16)
            for t in range(B):
                sp.wait_ge(T["v_sb"], t + 1)
                sp.dma_start(v_dram[t], v_sb[:, t, :]).then_inc(T["v_st"], 16)
                sp.wait_ge(T["v_st"], 16 * (t + 1))
                sp.dma_start(vs[:, t, :, :], v_dram[t].rearrange("(g t) (h e) -> (t h) g e", t=TG, h=H)).then_inc(T["v_ld"], 16)
            for t in range(B):
                sp.wait_ge(T["og"], t + 1)
                sp.dma_start(o_dram[t].rearrange("(g t) (h e) -> (t h) g e", t=TG, h=H), og[:, t, :, :]).then_inc(T["o_st"], 16)
                sp.wait_ge(T["o_st"], 16 * (t + 1))
                sp.dma_start(o2[:, t, :], o_dram[t]).then_inc(T["o_ld"], 16)
            for t in range(B):
                sp.wait_ge(T["fin"], t + 1)
                sp.dma_start(out[t * LQ:(t + 1) * LQ, :], fin[:, t, :]).then_inc(T["out"], 16)
            sp.wait_ge(T["out"], 16 * B)

        @block.tensor
        def _(pe):
            def x_transposed():
                pe.wait_ge(in_small, 32)
                for t in range(B):
                    pe.wait_ge(ln_out, t + 1)
                    for kt in range(KT):
                        last = pe.transpose(ps[:, 6 + t, kt * P:kt * P + P], xn0[:, t, kt * P:kt * P + P], id32[:, :])
                    last.then_inc(ln_t, 1)

            def project_q():
                pe.wait_ge(in_wq, 16)
                pe.wait_ge(ln_tc, B)
                for m in range(MT):
                    for kt in range(KT):
                        last = pe.matmul(ps[:, (0, 1, 6, 7)[m], 0:B * LQ], wq_sb[:, kt, m * P:m * P + P],
                                         xn0_t[:, kt, :, :].rearrange("p b q -> p (b q)"), start=kt == 0, stop=kt == KT - 1)
                    last.then_inc(q_mm, 1)

            def product(b, c, u, i, kt):
                n, s = unit_no(b, c, u), c % 2
                wh, xh = ((0, 0), (0, 1), (1, 0))[i]
                if u >= MT:
                    lhs = (c_lo if xh else c_hi)[:, s, kt, (u - MT) * P:(u - MT) * P + P]
                    rhs = (wv_lo if wh else wv_hi)[:, kt, :]
                else:
                    lhs = (wk_lo if wh else wk_hi)[:, kt, u * P:u * P + P]
                    rhs = (c_lo if xh else c_hi)[:, s, kt, :]
                return pe.matmul(ps[:, UB + n % 4, :], lhs, rhs, start=i == 0 and kt == 0, stop=i == 2 and kt == KT - 1)

            def project(b, c, u):
                n = unit_no(b, c, u)
                pe.wait_ge(unit_lo, n - 3)
                for i in range(3):
                    if u == 0 and i == 0:
                        pe.wait_ge(c_hi_set, b * NCH + c + 1)
                    if u == 0 and i == 1:
                        pe.wait_ge(c_lo_set, b * NCH + c + 1)
                    if n == MT:
                        pe.wait_ge(w_lo_set if i == 2 else w_hi_set, 2)
                    for kt in range(KT):
                        last = product(b, c, u, i, kt)
                last.then_inc(unit_mm, 1)

            def project_first():
                for kt in range(KT - 1):
                    pe.wait_ge(first_hi, 2 * (kt + 1))
                    for u in range(MT):
                        product(0, 0, u, 0, kt)
                    for n, i in enumerate((2, 1)):
                        pe.wait_ge(first_lo, 2 * kt + n + 1)
                        for u in range(MT):
                            product(0, 0, u, i, kt)
                pe.wait_ge(w_hi_set, 1)
                pe.wait_ge(c_hi_set, 1)
                for u in range(MT):
                    product(0, 0, u, 0, KT - 1)
                pe.wait_ge(c_lo_set, 1)
                pe.wait_ge(w_lo_set, 1)
                for u in range(MT):
                    for i in (1, 2):
                        last = product(0, 0, u, i, KT - 1)
                    last.then_inc(unit_mm, 1)

            def project_ahead(b, u):
                pe.wait_ge(c_hi_set, b * NCH + 1)
                pe.wait_ge(p_exp, 4 * H * b - (2 if u == 0 else 0))
                for i in range(2):
                    if i == 1:
                        pe.wait_ge(c_lo_set, b * NCH + 1)
                    for v in (u, u + 1):
                        for kt in range(KT):
                            product(b, 0, v, i, kt)

            def project_rest(b, u):
                pe.wait_ge(wk_lo_back, 16)
                for kt in range(KT):
                    last = product(b, 0, u, 2, kt)
                last.then_inc(unit_mm, 1)

            def scores(b, h, pair):
                g = b * H + h
                if pair == 0:
                    pe.wait_ge(k_stacked[h % NSLOT], 48 * (g // NSLOT + 1))
                    if h < NSLOT:
                        pe.wait_ge(ones_set, NSLOT * b + h + 1)
                    if h == 0:
                        pe.wait_ge(zeros_set, b + 1)
                for i in (2 * pair, 2 * pair + 1):
                    s = 4 * g + i
                    if s >= 2:
                        pe.wait_ge(s_max, s - 1)
                    pe.matmul(ps[:, s % 2, :], q_stack[:, h, :], k_slot(h)[:, i * CH:(i + 1) * CH],
                              start=True, stop=True).then_inc(s_mm, 1)

            def max_row(b, h):
                g = b * H + h
                pe.wait_ge(m_lo, g + 1)
                if g:
                    pe.wait_ge(m_row, g)
                pe.matmul(ps[:, 7, 0:P], m_cols[:, g % 2, :], id_r[:, :], start=True, stop=True).then_inc(m_mm, 1)

            def scores_t(b, h, i):
                g = b * H + h
                x_ = 2 * g + i
                if i == 0:
                    pe.wait_ge(m_row, g + 1)
                if x_ >= 2:
                    pe.wait_ge(p_exp, 2 * (x_ - 1))
                for k in range(HALF):
                    kt = i * HALF + k
                    last = pe.matmul(ps[:, 2 + 2 * (x_ % 2) + k // 4, (k % 4) * LQ:(k % 4) * LQ + LQ],
                                     k_slot(h)[:, kt * P:kt * P + P], q_stack[:, h, :], start=True, stop=True)
                last.then_inc(st_mm, 1)

            def weighted(b, h, i):
                g = b * H + h
                x_ = 2 * g + i
                if g % HPT == 0 and i == 0 and g:
                    pe.wait_ge(acc_read, 2 * (g // HPT))
                col = (h % HPT) * VC
                if i == 0:
                    pe.wait_ge(low_dve, g + 1)
                pe.wait_ge(low_pool, x_ + 1)
                for k in range(HALF):
                    kt = i * HALF + k
                    pe.matmul(ps[:, 6, col:col + VC], p_hi[:, x_ % 3, k * LQ:k * LQ + LQ],
                              v_parts[:, kt, h, :], start=kt == 0, stop=False)
                    last = pe.matmul(ps[:, 6, col + HD:col + VC], p_lo[:, x_ % 3, k * LQ:k * LQ + LQ],
                                     v_parts[:, kt, h, HD:VC], start=False, stop=kt == NKT - 1)
                last.then_inc(pv_mm, 1)

            def gemm(o, lhs, rhs):
                for kt in range(KT):
                    last = pe.matmul(o, lhs(kt), rhs(kt), start=kt == 0, stop=kt == KT - 1)
                return last

            def transposes(t, src, done):
                for kt in range(KT):
                    last = pe.transpose(ps[:, t, kt * P:kt * P + P], src[:, t, kt * P:kt * P + P], id32[:, :])
                last.then_inc(done, 1)

            def output_product(t):
                pe.wait_ge(T["in_wo"], 16)
                pe.wait_ge(T["a_tc"], t + 1)
                gemm(ps[:, (1, 3)[t], :], lambda kt: a_tt[:, t, kt, :], lambda kt: wo_sb[:, kt, :]).then_inc(T["y"], 1)

            for b in range(B):
                for c in range(NCH):
                    for u in range(UNITS):
                        if b == 0 and c == 0 and u == 0:
                            project_first()
                        if b and c == 0 and u < MT:
                            project_rest(b, u)
                        elif c or u >= MT:
                            project(b, c, u)
                        if b == 0 and c == 0 and u == MT + 2:
                            x_transposed()
                        if b == 0 and c == 0 and u == UNITS - 1:
                            project_q()
                        if c == NCH - 1 and u == MT:
                            pe.wait_ge(q_stacked, 16 * 12 * (b + 1))
                            scores(b, 0, 0)
                        if c == NCH - 1 and u == MT + 1:
                            scores(b, 0, 1)
                        if c == NCH - 1 and u == MT + 2:
                            max_row(b, 0)
                            scores(b, 1, 0)
                pe.wait_ge(unit_lo, (b + 1) * NCH * UNITS - 2)
                scores_t(b, 0, 0)
                scores(b, 1, 1)
                pe.wait_ge(unit_lo, (b + 1) * NCH * UNITS)
                scores_t(b, 0, 1)
                scores(b, 2, 0)
                max_row(b, 1)
                scores(b, 2, 1)
                pe.wait_ge(v_low, (b + 1) * NCH * TT)
                pe.wait_ge(const_set, 1)
                for h in range(1, H):
                    for i in range(2):
                        scores_t(b, h, i)
                        if b == B - 1 and h == H - 1 and i == 0:
                            pe.wait_ge(s_max, 4 * B * H)
                            pe.wait_ge(T["a"], 1)
                            transposes(0, a_t, T["a_tr"])
                        if h + 2 < H:
                            scores(b, h + 2, i)
                        if b == B - 1 and h == H - 1 and i == 1:
                            output_product(0)
                        weighted(b, h - 1, i)
                        if i == 0 and h + 1 < H:
                            max_row(b, h + 1)
                for i in range(2):
                    if b < B - 1:
                        project_ahead(b + 1, 2 * i)
                    weighted(b, H - 1, i)

            def mixing_transposes(t, src, bank, done):
                for m in range(MT):
                    last = pe.transpose(ps[:, bank, m * P:m * P + P], src[:, t, m * P:m * P + P], id32[:, :])
                last.then_inc(done, 1)

            def split_product(t, x_hi, x_lo, hi_set, lo_set, name, bank):
                hi, lo = high_halves[name], low_halves[name]
                pe.wait_ge(hi_set, t + 1)
                pe.wait_ge(T[name + "_hi"], 1)
                for i, (x_, w) in enumerate(((x_hi, hi), (x_lo, hi), (x_hi, lo))):
                    if i == 1:
                        pe.wait_ge(lo_set, t + 1)
                    if i == 2:
                        pe.wait_ge(T[name + "_lo"], 1)
                    for kt in range(KT):
                        last = pe.matmul(ps[:, bank, :], x_[:, t, kt, :], w[:, kt, :], start=i == 0 and kt == 0,
                                         stop=i == 2 and kt == KT - 1)
                return last

            def values(t):
                split_product(t, xn1_hi, xn1_lo, T["tc"], T["x_lo"], "w_v", (4, 7)[t]).then_inc(T["v_mm"], 1)

            def keys_queries(t, i):
                if t:
                    pe.wait_ge(T["x_lo"], i + 1)
                split_product(t, xn1_hi, xn1_lo, T["tc"], T["x_lo"], ("w_k", "w_q")[i], ((5, 6), (0, 1))[t][i]).then_inc(T["kq_mm"], 1)

            def head_product(t, g):
                n = t * (NG // 4) + g // 4
                if g == 0:
                    pe.wait_ge(T["q_tc"], 4 * t + 4)
                    pe.wait_ge(T["k_tc"], 4 * t + 4)
                if g % 4 == 0 and n >= 2:
                    pe.wait_ge(T["g_m"], n - 1)
                mm = pe.matmul(ps[:, 5 + n % 2, (g % 4) * P:(g % 4) * P + P],
                               k_t[:, t, g * TG:(g + 1) * TG, :].rearrange("p t h -> p (t h)"),
                               q_t[:, t, g * TG:(g + 1) * TG, :].rearrange("p t h -> p (t h)"), start=True, stop=True)
                if g % 4 == 3:
                    mm.then_inc(T["g_mm"], 1)

            def mixed(t, g):
                if g == 0:
                    pe.wait_ge(T["v_ld"], 16 * (t + 1))
                if g % 4 == 0:
                    pe.wait_ge(T["g_m"], t * (NG // 4) + g // 4 + 1)
                mm = pe.matmul(ps[:, (4, 7)[t], g * HD:(g + 1) * HD], g_m[:, t, g, :], vs[:, t, g, :], start=True, stop=True)
                if g == NG - 1:
                    mm.then_inc(T["o_mm"], 1)

            def second_transposed(t):
                pe.wait_ge(T["xn2"], t + 1)
                transposes(t, xn2, T["tr2"])

            def channel_keys(t):
                pe.wait_ge(T["in_f_k"], 16)
                for m in range(MT):
                    for kt in range(KT):
                        if m == 0:
                            pe.wait_ge(T["mix_k"], KT * t + kt + 1)
                        last = pe.matmul(ps[:, 2 + t, m * LQ:m * LQ + LQ], f_k_sb[:, kt, m * P:m * P + P], xk[:, kt, t, :],
                                         start=kt == 0, stop=kt == KT - 1)
                last.then_inc(T["k_mm"], 1)

            def channel_gate(t):
                split_product(t, xr_hi, xr_lo, T["xr_hi"], T["xr_lo"], "f_r", (4, 7)[t]).then_inc(T["r_mm"], 1)

            def channel_values(t):
                split_product(t, ka_hi, ka_lo, T["ka_hi"], T["ka_lo"], "f_v", 5 + t).then_inc(T["f_mm"], 1)

            def first_transposed(t):
                pe.wait_ge(T["xn"], t + 1)
                transposes(t, xn1, T["tr"])

            first_transposed(0)
            pe.wait_ge(T["a"], 2)
            transposes(1, a_t, T["a_tr"])
            keys_queries(0, 0)
            output_product(1)
            keys_queries(0, 1)
            first_transposed(1)
            values(0)
            keys_queries(1, 0)
            pe.wait_ge(T["soft"], 1)
            mixing_transposes(0, sk, 3, T["kt_mm"])
            pe.wait_ge(T["soft"], 2)
            mixing_transposes(0, sq, 2, T["qt_mm"])
            keys_queries(1, 1)
            values(1)
            for g in range(NG):
                head_product(0, g)
            pe.wait_ge(T["k_tc"], HPT)
            pe.wait_ge(T["soft"], 3)
            mixing_transposes(1, sk, 3, T["kt_mm"])
            pe.wait_ge(T["soft"], 4)
            mixing_transposes(1, sq, 2, T["qt_mm"])
            for g in range(NG):
                mixed(0, g)
            for g in range(NG):
                head_product(1, g)
            for g in range(NG):
                mixed(1, g)
            second_transposed(0)
            channel_keys(0)
            channel_gate(0)
            second_transposed(1)
            channel_values(0)
            channel_keys(1)
            channel_gate(1)
            channel_values(1)

        @block.scalar
        def _(act):
            def chunk_hi(n):
                act.wait_ge(in_chunk, 16 * n)
                if n % NCH >= 2:
                    act.wait_ge(unit_mm, (n - 1) * UNITS)
                elif n >= NCH:
                    act.wait_ge(low_dve, n // NCH * H)
                    act.wait_ge(low_pool, 2 * (n // NCH * H))
                act.activation(c_hi[:, n % 2, :, :], c_raw[:, :, :], ACT.Copy).then_inc(c_hi_set, 1)

            def x_std():
                act.wait_ge(eps_set, 1)
                for t in range(B):
                    act.wait_ge(ln_stat, t + 1)
                    act.activation(std[:, t:t + 1], mv[:, t, 1:2], ACT.Sqrt, bias=eps[:, :]).then_inc(ln_std, 1)

            def x_transposed():
                for t in range(B):
                    act.wait_ge(ln_t, t + 1)
                    act.activation(xn0_t[:, :, t, :], ps[:, 6 + t, :].rearrange("p (k q) -> p k q", k=KT), ACT.Copy).then_inc(ln_tc, 1)

            def project_q():
                for m in range(MT):
                    act.wait_ge(q_mm, m + 1)
                    act.activation(qa[:, :, m * P:m * P + P],
                                   ps[:, (0, 1, 6, 7)[m], 0:B * LQ].rearrange("p (b q) -> p b q", b=B),
                                   ACT.Identity, bias=colt[:, 0, m:m + 1]).then_inc(q_out, 1)
                act.wait_ge(q_out, MT)

            def q_high(b):
                if b:
                    act.wait_ge(pv_mm, 2 * H * b)
                act.activation(q_hi[:, :], qa[:, b, :], ACT.Copy).then_inc(q_hi_set, 1)

            def v_middle(n):
                v = v_units(n)
                act.wait_ge(unit_lo, n + 1)
                act.activation(v_parts[:, v % NKT, :, 2 * HD:3 * HD],
                               r1[:, v % 2, :].rearrange("p (h e) -> p h e", h=H), ACT.Copy).then_inc(v_mid, 1)

            def exps(g, i):
                x_ = 2 * g + i
                act.wait_ge(st_mm, x_ + 1)
                src = ps[:, 2 + 2 * (x_ % 2):4 + 2 * (x_ % 2), :].rearrange("p b c -> p (b c)")
                if g:
                    if i == 0:
                        act.wait_ge(low_dve, g)
                    act.wait_ge(low_pool, x_ - 1)
                act.activation(p_full[:, x_ % 2, :], src, ACT.Exp, scale=SCALE).then_inc(p_exp, 1)
                if x_ >= 3:
                    act.wait_ge(pv_mm, x_ - 2)
                act.activation(p_hi[:, x_ % 3, :], src, ACT.Exp, scale=SCALE).then_inc(p_exp, 1)

            def max_row(b, h):
                g = b * H + h
                act.wait_ge(m_mm, g + 1)
                act.activation(q_stack[SR:P, h, :], ps[SR:P, 7, 0:LQ], ACT.Copy).then_inc(m_row, 1)

            for kt in range(KT):
                act.wait_ge(in_first[kt], 32)
                act.activation(wk_hi[:, kt, :], w_raw[:, 0, kt, :], ACT.Copy).then_inc(first_hi if kt < KT - 1 else w_hi_set, 1)
                act.activation(c_hi[:, 0, kt, :], c_raw[:, kt, :], ACT.Copy).then_inc(first_hi if kt < KT - 1 else c_hi_set, 1)
            act.wait_ge(in_wv, 16)
            act.activation(wv_hi[:, :, :], w_raw[:, 1, :, :], ACT.Copy).then_inc(w_hi_set, 1)
            act.wait_ge(in_small, 32)
            for b in range(B):
                if b:
                    q_high(b)
                for c in range(NCH):
                    for u in range(UNITS):
                        n = unit_no(b, c, u)
                        if c == NCH - 1 and u == MT:
                            if b:
                                act.wait_ge(exp_loaded, b)
                            act.activation(warm[:, :], eps[:, :], ACT.Exp).then_inc(exp_loaded, 1)
                        if c == NCH - 1 and u == UNITS - 1:
                            max_row(b, 0)
                        act.wait_ge(unit_mm, n + 1)
                        if u >= MT:
                            if n == MT:
                                act.wait_ge(w_lo_set, 2)
                            act.activation(v_parts[:, c * TT + u - MT, :, HD:2 * HD],
                                           ps[:, UB + n % 4, :].rearrange("p (h e) -> p h e", h=H), ACT.Copy).then_inc(unit_hi, 1)
                            if u > MT:
                                v_middle(n - 1)
                            if u == UNITS - 1:
                                v_middle(n)
                        else:
                            act.activation(k_hi[:, u, c * CH:(c + 1) * CH], ps[:, UB + n % 4, :], ACT.Identity,
                                           bias=colt[:, 1, u:u + 1]).then_inc(unit_hi, 1)
                        if b == 0 and c == 0 and u == MT - 1:
                            x_std()
                        if b == 0 and c == 0 and u == MT + 2:
                            x_transposed()
                        if b == 0 and c == 0 and u == UNITS - 1:
                            project_q()
                            q_high(0)
                        if u == 1 and c + 1 < NCH:
                            chunk_hi(b * NCH + c + 1)
                exps(b * H, 0)
                max_row(b, 1)
                exps(b * H, 1)
                for h in range(1, H):
                    exps(b * H + h, 0)
                    if h + 1 < H:
                        max_row(b, h + 1)
                    exps(b * H + h, 1)

            warmed = [B]

            def load_table(func):
                act.wait_ge(exp_loaded, warmed[0])
                act.activation(warm[:, :], eps[:, :], func).then_inc(exp_loaded, 1)
                warmed[0] += 1

            def layer_std(t, stat_done, done):
                act.wait_ge(stat_done, t + 1)
                act.activation(std[:, t:t + 1], mv[:, t, 1:2], ACT.Sqrt, bias=eps[:, :]).then_inc(done, 1)

            def key_query_exp(t, i):
                act.wait_ge(T["sub"], 2 * t + i + 1)
                s_ = (sk, sq)[i]
                act.activation(s_[:, t, :], s_[:, t, :], ACT.Exp).then_inc(T["exp"], 1)

            def v_out(t):
                act.wait_ge(T["v_mm"], t + 1)
                act.activation(v_sb[:, t, :], ps[:, (4, 7)[t], :], ACT.Copy).then_inc(T["v_sb"], 1)

            def rows_of(t, bank, dst, transposed, done):
                act.wait_ge(transposed, t + 1)
                for j in range(HPT):
                    act.activation(dst[0:HD, t, :, :].rearrange("p q (m j) -> p j m q", j=HPT)[:, j, :, :],
                                   ps[HD * j:HD * j + HD, bank, :].rearrange("p (m q) -> p m q", m=MT), ACT.Copy).then_inc(done, 1)

            def key_rows(t):
                rows_of(t, 3, k_t, T["kt_mm"], T["k_tc"])

            def query_rows(t):
                rows_of(t, 2, q_t, T["qt_mm"], T["q_tc"])

            def mixed_out(t):
                act.wait_ge(T["o_mm"], t + 1)
                act.activation(og[:, t, :, :].rearrange("p g e -> p (g e)"), ps[:, (4, 7)[t], :], ACT.Copy).then_inc(T["og"], 1)

            def positive(t):
                act.wait_ge(T["k_mm"], t + 1)
                act.activation(relu[:, t, :, :], ps[:, 2 + t, :].rearrange("p (m q) -> p m q", m=MT), ACT.Relu).then_inc(T["relu"], 1)

            def first_out(t):
                act.wait_ge(T["tr"], t + 1)
                act.activation(xn1_hi[:, t, :, :].rearrange("p k q -> p (k q)"), ps[:, t, :], ACT.Copy).then_inc(T["tc"], 1)

            def weight_high(name, raw):
                act.wait_ge(T["in_" + name], 16)
                act.activation(high_halves[name][:, :, :], raw[:, :, :], ACT.Copy).then_inc(T[name + "_hi"], 1)

            load_table(ACT.Sqrt)
            layer_std(0, T["ln"], T["std"])
            first_out(0)
            act.wait_ge(T["a_tr"], 2)
            act.activation(a_tt[:, 1, :, :].rearrange("p k q -> p (k q)"), ps[:, 1, :], ACT.Copy).then_inc(T["a_tc"], 1)
            weight_high("w_q", w_q_sb)
            weight_high("w_v", w_v_sb)
            layer_std(1, T["ln"], T["std"])
            load_table(ACT.Exp)
            key_query_exp(0, 0)
            first_out(1)
            key_query_exp(0, 1)
            v_out(0)
            act.wait_ge(T["rows_zero"], 2)
            key_rows(0)
            key_query_exp(1, 0)
            query_rows(0)
            key_query_exp(1, 1)
            load_table(ACT.Sqrt)
            v_out(1)
            act.wait_ge(T["rows_zero"], 2 * B)
            key_rows(1)
            query_rows(1)
            mixed_out(0)
            weight_high("f_r", f_r_sb)
            act.wait_ge(T["y"], B)
            weight_high("f_v", f_v_sb)
            layer_std(0, T["ln2"], T["std2"])
            mixed_out(1)
            act.wait_ge(T["zero"], 1)
            act.wait_ge(T["om"], 1)
            for t in range(B):
                if t:
                    layer_std(t, T["ln2"], T["std2"])
                    load_table(ACT.Sigmoid)
                    positive(0)
                act.wait_ge(T["tr2"], t + 1)
                act.activation(xp_t[:, :, t, 1:LQ + 1], ps[:, t, :].rearrange("p (k q) -> p k q", k=KT), ACT.Copy).then_inc(T["xp"], 1)
                act.wait_ge(T["xp"], t + 1)
                for i in (1, 0):
                    for kt in range(KT):
                        act.activation(prev[:, i, kt, t, :], xp_t[:, kt, t, 0:LQ], ACT.Copy, scale=om[:, i, kt:kt + 1]).then_inc(T["prev"], 1)
                act.wait_ge(T["mix_r"], KT * (t + 1))
                act.activation(xr_hi[:, t, :, :], xr[:, t, :, :], ACT.Copy).then_inc(T["xr_hi"], 1)
            for t in range(B):
                if t:
                    positive(t)
                act.wait_ge(T["r_mm"], t + 1)
                act.activation(gate[:, t, :], ps[:, (4, 7)[t], :], ACT.Sigmoid).then_inc(T["gate"], 1)

        @block.vector
        def _(dve):
            chain = [0]

            def link(ins):
                chain[0] += 1
                ins.then_inc(dve_chain, 1)
                dve.wait_ge(dve_chain, chain[0])

            def chunk_lo(n):
                dve.wait_ge(c_hi_set, n + 1)
                if n // NCH and n % NCH == 0:
                    dve.wait_ge(st_mm, 2 * (n // NCH * H - NSLOT + 3))
                elif n // NCH and n % NCH == 1:
                    dve.wait_ge(pv_mm, 2 * H * (n // NCH))
                dve.tensor_tensor(c_lo[:, n % 2, :, :], c_raw[:, :, :], c_hi[:, n % 2, :, :].bitcast(F32),
                                  ALU.subtract).then_inc(c_lo_set, 1)

            def x_stats():
                dve.wait_ge(in_x, 16)
                for t in range(B):
                    link(dve.bn_stats(stat[:, t, :], x_in[:, t, :]))
                    dve.bn_aggr(mv[:, t, :], stat[:, t, :]).then_inc(ln_stat, 1)

            def x_norm():
                dve.wait_ge(ln_stat, B)
                for t in range(B):
                    dve.wait_ge(ln_std, t + 1)
                    link(dve.reciprocal(rstd[:, t:t + 1], std[:, t:t + 1]))
                    dve.tensor_scalar(xn0[:, t, :], x_in[:, t, :], mv[:, t, 0:1], rstd[:, t:t + 1],
                                      ALU.subtract, ALU.mult).then_inc(ln_out, 1)
                dve.wait_ge(in_small, 32)
                link(dve.tensor_copy(id_r[:, :], id32[:, :]))

            def next_chunk_hi(b):
                n = (b + 1) * NCH
                dve.wait_ge(in_chunk, 16 * n)
                dve.wait_ge(st_mm, 2 * ((b + 1) * H - NSLOT + 2))
                dve.tensor_copy(c_hi[:, 0, :, :], c_raw[:, :, :]).then_inc(c_hi_set, 1)

            def q_low(b):
                dve.wait_ge(q_hi_set, b + 1)
                dve.tensor_tensor(q_lo[:, :], qa[:, b, :], q_hi[:, :].bitcast(F32), ALU.subtract).then_inc(q_lo_set, 1)

            def maxima(b, h, pair):
                g = b * H + h
                if g and pair == 0:
                    dve.wait_ge(m_lo, g)
                for i in (2 * pair, 2 * pair + 1):
                    dve.wait_ge(s_mm, 4 * g + i + 1)
                    dve.tensor_reduce(pm[:, i:i + 1], ps[:, (4 * g + i) % 2, :], AX_X, ALU.max).then_inc(s_max, 1)

            def maximum(b, h):
                g = b * H + h
                dve.wait_ge(s_max, 4 * g + 4)
                dve.tensor_reduce(m_q[:, :], pm[:, :], AX_X, ALU.max).then_inc(m_red, 1)
                dve.wait_ge(m_red, g + 1)
                if g >= 2:
                    dve.wait_ge(m_mm, g - 1)
                dve.tensor_scalar(m_cols[:, g % 2, SR:SR + 1], m_q[:, :], -1.0, LIFT, ALU.mult, ALU.add).then_inc(m_hi, 1)
                dve.tensor_scalar(pm[:, 0:1], m_q[:, :], -1.0, LIFT, ALU.mult, ALU.add).then_inc(m_hi, 1)
                dve.wait_ge(m_hi, 2 * g + 2)
                dve.tensor_tensor(m_cols[:, g % 2, SR + 1:SR + 2], pm[:, 0:1],
                                  m_cols[:, g % 2, SR:SR + 1].bitcast(F32), ALU.subtract).then_inc(m_lo, 1)

            def lows(b, h):
                x_ = 2 * (b * H + h)
                dve.wait_ge(p_exp, 2 * (x_ + 1))
                if x_ >= 3:
                    dve.wait_ge(pv_mm, x_ - 2)
                dve.tensor_tensor(p_lo[:, x_ % 3, 0:DF], p_full[:, 0, 0:DF], p_hi[:, x_ % 3, 0:DF], ALU.subtract).then_inc(low_dve, 1)

            def gather(b, m):
                k = b * MT + m
                dve.wait_ge(pv_mm, 2 * HPT * (k + 1))
                acc = ps[:, 6, 0:HPT * VC].rearrange("p (j c) -> p j c", j=HPT)
                dst = qa[:, b, m * P:m * P + P].rearrange("p (j e) -> p j e", j=HPT)
                dve.tensor_reduce(dst, acc[:, :, 0:3 * HD].rearrange("p j (c e) -> p j e c", c=3), AX_X, ALU.add).then_inc(acc_read, 1)
                dve.reciprocal(rec[:, :], acc[:, :, VC - 1]).then_inc(acc_read, 1)

            def weigh(b, m):
                k = b * MT + m
                dve.wait_ge(acc_read, 2 * (k + 1))
                dst = qa[:, b, m * P:m * P + P].rearrange("p (j e) -> p j e", j=HPT)
                dve.tensor_tensor(dst, dst, rec[:, :].unsqueeze(2).to_broadcast([P, HPT, HD]), ALU.mult).then_inc(a_out, 1)
                dve.wait_ge(a_out, k + 1)

            def with_bias(t):
                dve.tensor_tensor(a_t[:, t, :], qa[:, t, :], bias_rows[:, 0, :], ALU.add).then_inc(T["a"], 1)

            def first_residual(t):
                dve.wait_ge(T["y"], t + 1)
                link(dve.tensor_tensor(x1[:, t, :], ps[:, (1, 3)[t], :], xo[:, t, :], ALU.add))
                statistics(t, x1, T["ln"])

            def statistics(t, src, stat_done):
                link(dve.bn_stats(stat[:, t, :], src[:, t, :]))
                dve.bn_aggr(mv[:, t, :], stat[:, t, :]).then_inc(stat_done, 1)

            def normalise(t, src, dst, stat_done, std_done, out_done):
                dve.wait_ge(stat_done, t + 1)
                dve.wait_ge(std_done, t + 1)
                link(dve.reciprocal(rstd[:, t:t + 1], std[:, t:t + 1]))
                dve.tensor_scalar(dst[:, t, :], src[:, t, :], mv[:, t, 0:1], rstd[:, t:t + 1],
                                  ALU.subtract, ALU.mult).then_inc(out_done, 1)

            def groups(t, i):
                bank = ((5, 6), (0, 1))[t][i]
                pattern = ("p (h e) -> p e h", "p (h e) -> p h e")[i]
                c = (slice(0, HD), slice(HD, HD + H))[i]
                return ps[:, bank, :].rearrange(pattern, h=H), (sk, sq)[i][:, t, :].rearrange(pattern, h=H), c

            def spread(a, n):
                return a.unsqueeze(2).to_broadcast([P, a.shape[1], n])

            def x_low(t):
                dve.wait_ge(T["tc"], t + 1)
                dve.tensor_tensor(xn1_lo[:, t, :, :].rearrange("p k q -> p (k q)"), ps[:, t, :],
                                  xn1_hi[:, t, :, :].rearrange("p k q -> p (k q)").bitcast(F32), ALU.subtract).then_inc(T["x_lo"], 1)

            def less_maximum(t, i):
                dve.wait_ge(T["kq_mm"], 2 * t + i + 1)
                src, dst, c = groups(t, i)
                link(dve.tensor_reduce(mx[:, t, c], src, AX_X, ALU.max))
                dve.tensor_tensor(dst, src, spread(mx[:, t, c], src.shape[2]), ALU.subtract).then_inc(T["sub"], 1)

            def by_sum(t, i):
                dve.wait_ge(T["exp"], 2 * t + i + 1)
                src, dst, c = groups(t, i)
                link(dve.tensor_reduce(sm[:, t, c], dst, AX_X, ALU.add))
                link(dve.reciprocal(rs[:, t, c], sm[:, t, c]))
                dve.tensor_tensor(dst, dst, spread(rs[:, t, c], dst.shape[2]), ALU.mult).then_inc(T["soft"], 1)

            def masked(t, i):
                n = t * (NG // 4) + i
                dve.wait_ge(T["g_mm"], n + 1)
                dve.tensor_tensor(g_m[:, t, 4 * i:4 * i + 4, :].rearrange("p g c -> p (g c)"), ps[:, 5 + n % 2, :],
                                  maskt[:, :, :].rearrange("p g c -> p (g c)"), ALU.mult).then_inc(T["g_m"], 1)

            def second_residual(t):
                dve.wait_ge(T["o_ld"], 16 * (t + 1))
                dve.tensor_tensor(x2[:, t, :], x1[:, t, :], o2[:, t, :], ALU.add).then_inc(T["x2"], 1)
                dve.wait_ge(T["x2"], t + 1)
                statistics(t, x2, T["ln2"])
                normalise(t, x2, xn2, T["ln2"], T["std2"], T["xn2"])

            def token_shift(t):
                dve.wait_ge(T["xp"], t + 1)
                dve.wait_ge(T["g_mm"], B * NG // 4)
                for n, (i, dst, done) in enumerate(((1, xk[:, :, t, :], T["mix_k"]), (0, xr[:, t, :, :], T["mix_r"]))):
                    for kt in range(KT):
                        dve.wait_ge(T["prev"], (2 * t + n) * KT + kt + 1)
                        dve.scalar_tensor_tensor(dst[:, kt, :], xp_t[:, kt, t, 1:LQ + 1], colt[:, 2 + i, kt:kt + 1],
                                                 prev[:, i, kt, t, :], ALU.mult, ALU.add).then_inc(done, 1)

                dve.wait_ge(T["xr_hi"], t + 1)
                dve.tensor_tensor(xr_lo[:, t, :, :], xr[:, t, :, :], xr_hi[:, t, :, :].bitcast(F32), ALU.subtract).then_inc(T["xr_lo"], 1)

            def squared_relu(t):
                dve.wait_ge(T["relu"], t + 1)
                dve.tensor_tensor(ka_hi[:, t, :, :], relu[:, t, :, :], relu[:, t, :, :], ALU.mult).then_inc(T["ka_hi"], 1)
                dve.tensor_tensor(ka[:, t, :, :], relu[:, t, :, :], relu[:, t, :, :], ALU.mult).then_inc(T["ka"], 1)
                dve.wait_ge(T["ka_hi"], t + 1)
                dve.wait_ge(T["ka"], t + 1)
                dve.tensor_tensor(ka_lo[:, t, :, :], ka[:, t, :, :], ka_hi[:, t, :, :].bitcast(F32), ALU.subtract).then_inc(T["ka_lo"], 1)

            def final(t):
                dve.wait_ge(T["gate"], t + 1)
                dve.wait_ge(T["f_mm"], t + 1)
                link(dve.tensor_tensor(fin[:, t, :], ps[:, 5 + t, :], gate[:, t, :], ALU.mult))
                dve.tensor_tensor(fin[:, t, :], fin[:, t, :], x2[:, t, :], ALU.add).then_inc(T["fin"], 1)

            dve.memset(eps[:, :], EPS).then_inc(eps_set, 1)
            for kt in range(KT):
                ends = kt == KT - 1
                dve.wait_ge(w_hi_set if ends else first_hi, 1 if ends else 2 * kt + 1)
                dve.tensor_tensor(wk_lo[:, kt, :], w_raw[:, 0, kt, :], wk_hi[:, kt, :].bitcast(F32),
                                  ALU.subtract).then_inc(w_lo_set if ends else first_lo, 1)
                dve.wait_ge(c_hi_set if ends else first_hi, 1 if ends else 2 * kt + 2)
                dve.tensor_tensor(c_lo[:, 0, kt, :], c_raw[:, kt, :], c_hi[:, 0, kt, :].bitcast(F32),
                                  ALU.subtract).then_inc(c_lo_set if ends else first_lo, 1)
            dve.wait_ge(w_hi_set, 2)
            dve.tensor_tensor(wv_lo[:, :, :], w_raw[:, 1, :, :], wv_hi[:, :, :].bitcast(F32), ALU.subtract).then_inc(w_lo_set, 1)
            x_stats()
            dve.wait_ge(in_small, 32)
            for b in range(B):
                if b:
                    gather(b - 1, MT - 1)
                    weigh(b - 1, MT - 1)
                    q_low(b)
                for c in range(NCH):
                    for u in range(UNITS):
                        n = unit_no(b, c, u)
                        dve.wait_ge(unit_hi, n + 1)
                        if u >= MT:
                            v = v_units(n)
                            if v >= 2:
                                dve.wait_ge(v_low, v - 1)
                            dve.tensor_tensor(r1[:, v % 2, :].rearrange("p (h e) -> p h e", h=H),
                                              ps[:, UB + n % 4, :].rearrange("p (h e) -> p h e", h=H),
                                              v_parts[:, v % NKT, :, HD:2 * HD], ALU.subtract).then_inc(unit_lo, 1)
                        else:
                            dve.scalar_tensor_tensor(k_lo[:, u, c * CH:(c + 1) * CH], ps[:, UB + n % 4, :], colt[:, 1, u:u + 1],
                                                     k_hi[:, u, c * CH:(c + 1) * CH].bitcast(F32),
                                                     ALU.add, ALU.subtract).then_inc(unit_lo, 1)
                        if b == 0 and c == 0 and u == MT - 1:
                            x_norm()
                        if b == 0 and c == 0 and u == UNITS - 1:
                            q_low(0)
                        if u == 1 and c + 1 < NCH:
                            chunk_lo(b * NCH + c + 1)
                        if c == NCH - 1 and u >= MT:
                            if b == 0:
                                dve.wait_ge(const_set, 2)
                            h, pair = (u - MT) // 2, (u - MT) % 2
                            maxima(b, h, pair)
                            if pair:
                                maximum(b, h)
                for h in range(H):
                    if h + 2 < H:
                        maxima(b, h + 2, 0)
                    if h + 2 < H:
                        maxima(b, h + 2, 1)
                    if b == B - 1 and h == H - 2:
                        dve.wait_ge(T["in_rows"], 16)
                        with_bias(0)
                    if b == B - 1 and h == H - 1:
                        dve.wait_ge(T["a_tr"], 1)
                        dve.wait_ge(T["in_wo"], 16)
                        dve.tensor_copy(a_tt[:, 0, :, :].rearrange("p k q -> p (k q)"), ps[:, 0, :]).then_inc(T["a_tc"], 1)
                    lows(b, h)
                    if h and h % HPT == 0:
                        gather(b, h // HPT - 1)
                    if h + 2 < H:
                        maximum(b, h + 2)
                    if h and h % HPT == 0:
                        weigh(b, h // HPT - 1)
                    if b == B - 1 and h == H - 2:
                        dve.wait_ge(T["in_x"], 16)
                        dve.wait_ge(T["in_rows"], 16)
                        for t in range(B):
                            link(dve.tensor_tensor(xo[:, t, :], x_res[:, t, :], bias_rows[:, 1, :], ALU.add))
                        dve.wait_ge(T["in_w_k"], 16)
                        dve.wait_ge(st_mm, 2 * (B * H - NSLOT + 1))
                        dve.tensor_copy(high_halves["w_k"][:, :, :], w_k_sb[:, :, :]).then_inc(T["w_k_hi"], 1)
                    if b == B - 1 and h == H - 1:
                        first_residual(0)
                    if b < B - 1 and h == H - 2:
                        next_chunk_hi(b)
                        chunk_lo((b + 1) * NCH)
            normalise(0, x1, xn1, T["ln"], T["std"], T["xn"])
            gather(B - 1, MT - 1)
            weigh(B - 1, MT - 1)
            with_bias(1)
            x_low(0)
            dve.wait_ge(m_mm, B * H)
            less_maximum(0, 0)
            first_residual(1)
            normalise(1, x1, xn1, T["ln"], T["std"], T["xn"])
            by_sum(0, 0)
            less_maximum(0, 1)
            x_low(1)
            by_sum(0, 1)
            less_maximum(1, 0)
            by_sum(1, 0)
            less_maximum(1, 1)
            dve.wait_ge(T["in_mask"], 16)
            masked(0, 0)
            masked(0, 1)
            by_sum(1, 1)
            for i in range(2, NG // 4):
                masked(0, i)
            for i in range(NG // 4):
                masked(1, i)
            second_residual(0)
            token_shift(0)
            second_residual(1)
            squared_relu(0)
            token_shift(1)
            squared_relu(1)
            final(0)
            final(1)

        @block.gpsimd
        def _(pool):
            def v_lowest(n):
                v = v_units(n)
                pool.wait_ge(v_mid, v + 1)
                pool.tensor_tensor(v_parts[:, v % NKT, :, 0:HD], r1[:, v % 2, :].rearrange("p (h e) -> p h e", h=H),
                                   v_parts[:, v % NKT, :, 2 * HD:3 * HD], ALU.subtract).then_inc(v_low, 1)

            def ones(b, i):
                pool.memset(k_slot(i)[SR:P, :].bitcast(F32), 1.0).then_inc(ones_set, 1)
                pool.wait_ge(ones_set, NSLOT * b + i + 1)

            def weight_low(name, raw):
                pool.wait_ge(T[name + "_hi"], 1)
                pool.tensor_tensor(low_halves[name][:, :, :], raw[:, :, :], high_halves[name][:, :, :].bitcast(F32),
                                   ALU.subtract).then_inc(T[name + "_lo"], 1)

            for b in range(B):
                for c in range(NCH):
                    if c == 1:
                        if b:
                            pool.wait_ge(st_mm, 2 * H * b)
                        else:
                            pool.wait_ge(T["om"], 1)
                        pool.wait_ge(v_low, v_units(unit_no(b, c, 0)))
                        pool.memset(q_stack[SR:P, :, :].bitcast(F32), 0.0).then_inc(zeros_set, 1)
                        pool.wait_ge(zeros_set, b + 1)
                    if c == NCH - 1:
                        pool.wait_ge(c_lo_set, (b + 1) * NCH)
                        pool.wait_ge(unit_mm, unit_no(b, c, 0))
                        pool.wait_ge(v_low, v_units(unit_no(b, c, 0)))
                        for i in range(NSLOT - 1):
                            ones(b, i)
                        pool.wait_ge(wk_lo_kept, 16)
                        pool.wait_ge(unit_mm, unit_no(b, c, MT))
                        ones(b, NSLOT - 1)
                    for u in range(MT, UNITS):
                        v_lowest(unit_no(b, c, u))
                    if b == 0 and c == 0:
                        pool.wait_ge(q_mm, MT)
                        pool.wait_ge(v_low, TT)
                        pool.memset(v_parts[:, :, :, VC - 1], 1.0).then_inc(const_set, 1)
                        pool.memset(m_cols[:, :, :].bitcast(F32), 0.0).then_inc(const_set, 1)
                        pool.wait_ge(in_small, 32)
                        pool.tensor_scalar(om[:, :, :], colt[:, 2:4, :], -1.0, 1.0, ALU.mult, ALU.add).then_inc(T["om"], 1)
                for h in range(H):
                    for i, first in ((0, DF), (1, 0)):
                        x_ = 2 * (b * H + h) + i
                        pool.wait_ge(p_exp, 2 * (x_ + 1))
                        if x_ >= 3:
                            pool.wait_ge(pv_mm, x_ - 2)
                        pool.tensor_tensor(p_lo[:, x_ % 3, first:FH], p_full[:, i, first:FH], p_hi[:, x_ % 3, first:FH],
                                           ALU.subtract).then_inc(low_pool, 1)
            for name, raw in (("w_k", w_k_sb), ("w_q", w_q_sb), ("w_v", w_v_sb)):
                weight_low(name, raw)
                if name == "w_k":
                    pool.wait_ge(pv_mm, 2 * B * H)
                    pool.memset(k_t[:, 0, :, :], 0.0).then_inc(T["rows_zero"], 1)
            for dst in (q_t[:, 0, :, :], k_t[:, 1, :, :], q_t[:, 1, :, :]):
                pool.memset(dst, 0.0).then_inc(T["rows_zero"], 1)
            pool.wait_ge(T["v_mm"], B)
            pool.memset(xp_t[:, :, :, 0:1], 0.0).then_inc(T["zero"], 1)
            for name, raw in (("f_r", f_r_sb), ("f_v", f_v_sb)):
                weight_low(name, raw)


def kernel(**inputs):
    import numpy as np
    import concourse.bacc as bacc
    from concourse.bass_utils import run_bass_kernel_spmd

    a = {k: np.asarray(v) for k, v in inputs.items()}

    def tiles(w):
        return np.ascontiguousarray(w.reshape(KT, P, D).transpose(1, 0, 2))

    def col(v):
        return v.reshape(KT, P).T

    ctx_in = a["ctx_1024"].reshape(B * NCH, CH, KT, P).transpose(0, 3, 2, 1)
    block = np.kron(np.eye(TG, dtype=np.float32), np.ones((H, H), np.float32))
    data = {
        "x": a["x"].reshape(B * LQ, D),
        "ctx_t": ctx_in,
        "wq": tiles(a["L0_xattn_Wq"]), "wk": tiles(a["L0_xattn_Wk"]), "wv": tiles(a["L0_xattn_Wv"]),
        "wo": tiles(a["L0_xattn_Wo"]),
        "w_q": tiles(a["L0_attn_W_Q"].T), "w_k": tiles(a["L0_attn_W_K"].T), "w_v": tiles(a["L0_attn_W_V"].T),
        "f_r": tiles(a["L0_ffn_W_r"].T), "f_k": tiles(a["L0_ffn_W_k"].T), "f_v": tiles(a["L0_ffn_W_v"].T),
        "cols": np.stack([col(a["L0_xattn_bq"]), col(a["L0_xattn_bk"]), col(a["L0_ffn_mu_r"]), col(a["L0_ffn_mu_k"])], 1),
        "rows": np.broadcast_to(np.stack([a["L0_xattn_bv"], a["L0_xattn_bo"]])[None], (P, 2, D)),
        "ident": np.eye(P, dtype=np.float32),
        "mask": np.broadcast_to(block[:, None, :], (P, 4, P)),
    }
    nc = bacc.Bacc("TRN2", target_bir_lowering=False, num_devices=1)
    arrays, args = {}, []
    for name, v in data.items():
        v = np.ascontiguousarray(v)
        arrays[f"in_{name}"] = v
        args.append(nc.dram_tensor(f"in_{name}", v.shape, F32, kind="ExternalInput").ap())
    out = nc.dram_tensor("out", [B * LQ, D], F32, kind="ExternalOutput").ap()
    perceiver(nc, *args, out)
    r = run_bass_kernel_spmd(nc, [arrays], core_ids=[0])
    return r.results[0]["out"].reshape(B, LQ, D)
```
